# Optimizing a Trainium2 kernel written in Bass

```python
import numpy as np
import jax
import jax.numpy as jnp

def _softmax(x, axis=-1):
    return jax.nn.softmax(x, axis=axis)

def _gelu(x):
    return jax.nn.gelu(x, approximate=True)

def _silu(x):
    return jax.nn.silu(x)

def _sigmoid(x):
    return jax.nn.sigmoid(x)

def _layernorm(x, axis=-1, eps=1e-05):
    m = jnp.mean(x, axis=axis, keepdims=True)
    v = jnp.var(x, axis=axis, keepdims=True)
    return (x - m) / jnp.sqrt(v + eps)

def _scatter_add(tgt, idx, src, axis=0):
    return tgt.at[idx].add(src)

def _segment_sum(src, seg, n):
    return jax.ops.segment_sum(src, seg, n)
kernel_name = 'mk_flamingo_gated_d1_seqx_r2_091c78'

def setup_inputs(seed: int=0):
    np.random.seed(seed)
    _w = jnp.asarray

    def _rec_inputs():
        import jax
        import jax.numpy as jnp
        _rk = jax.random.key(seed)
        x = -0.0002928 + 1 * jax.random.normal(jax.random.fold_in(_rk, 1), (16, 256, 512), jnp.float32)
        _lenS = 256 - jax.random.randint(jax.random.fold_in(_rk, 7), (16,), 0, max(1, 256 // 4) + 1, jnp.int32)
        _lenS2 = 256 - jax.random.randint(jax.random.fold_in(_rk, 8), (16,), 0, max(1, 256 // 4) + 1, jnp.int32)
        _ctx_1024P = jax.random.normal(jax.random.fold_in(_rk, 11), (16, 16, 512), jnp.float32)
        _ctx_1024c = jax.random.dirichlet(jax.random.fold_in(_rk, 511), 0.3 * jnp.ones((16,), jnp.float32), (16, 256))
        _ctx_1024t = jnp.einsum('bsk,bkd->bsd', _ctx_1024c, _ctx_1024P)
        _ctx_1024t = _ctx_1024t * jax.lax.rsqrt(jnp.mean(jnp.square(_ctx_1024t)) + 1e-12) * 0.953939
        ctx_1024 = -0.000292821 + 1.00034 * (_ctx_1024t + 0.3 * jax.random.normal(jax.random.fold_in(_rk, 611), (16, 256, 512), jnp.float32))
        _g = jax.random.normal(jax.random.fold_in(_rk, 9001), (2, 1), jnp.float32)
        _g = jnp.sign(_g) * jnp.maximum(jnp.abs(_g), 1.0) + (_g == 0) * 1.0
        g_xattn = _g[0]
        g_ffn = _g[1]
        return (x, ctx_1024, g_xattn, g_ffn)
    x, ctx_1024, g_xattn, g_ffn = _rec_inputs()

    def _L0_xattn_setup():
        import jax, jax.numpy as jnp
        import numpy as np
        HIDDEN = 512
        HEADS = 16
        HEAD_DIM = HIDDEN // HEADS
        SCALE = 1.0 / np.sqrt(HEAD_DIM).astype(np.float32)
        key = jax.random.key(seed)
        ks = jax.random.split(key, 8)
        b, t = (2, 1024)
        x = jax.random.normal(ks[0], (b, t, HIDDEN), dtype=jnp.float32)
        context = x
        s = 0.02
        Wq = jax.random.normal(ks[1], (HIDDEN, HIDDEN), dtype=jnp.float32) * s
        Wk = jax.random.normal(ks[2], (HIDDEN, HIDDEN), dtype=jnp.float32) * s
        Wv = jax.random.normal(ks[3], (HIDDEN, HIDDEN), dtype=jnp.float32) * s
        Wo = jax.random.normal(ks[4], (HIDDEN, HIDDEN), dtype=jnp.float32) * s
        bo = jnp.zeros((HIDDEN,), dtype=jnp.float32)
        return {'x': x, 'context': context, 'Wq': Wq, 'Wk': Wk, 'Wv': Wv, 'Wo': Wo, 'bo': bo}
    _L0_xattn_all = _L0_xattn_setup()
    _L0_xattn_in = {k: v for k, v in _L0_xattn_all.items() if k in ('Wq', 'Wk', 'Wv', 'Wo', 'bo')}
    del _L0_xattn_all

    def _L0_ffn_setup():
        import jax, jax.numpy as jnp
        import numpy as np
        TOP_K = 6

        def _glu_mlp(x, wg, wu, wd):
            return jax.nn.silu(x @ wg) * (x @ wu) @ wd
        key = jax.random.key(seed)
        ks = jax.random.split(key, 8)
        B, S, D, E, F, FS = (2, 1024, 512, 8, 256, 512)
        sc = 0.02
        return {'hidden_states': jax.random.normal(ks[0], (B, S, D), jnp.float32), 'router_w': jax.random.normal(ks[1], (D, E), jnp.float32) * sc, 'w_gate': jax.random.normal(ks[2], (E, D, F), jnp.float32) * sc, 'w_up': jax.random.normal(ks[3], (E, D, F), jnp.float32) * sc, 'w_down': jax.random.normal(ks[4], (E, F, D), jnp.float32) * sc, 'ws_gate': jax.random.normal(ks[5], (D, FS), jnp.float32) * sc, 'ws_up': jax.random.normal(ks[6], (D, FS), jnp.float32) * sc, 'ws_down': jax.random.normal(ks[7], (FS, D), jnp.float32) * sc}
    _L0_ffn_all = _L0_ffn_setup()
    _L0_ffn_in = {k: v for k, v in _L0_ffn_all.items() if k in ('router_w', 'w_gate', 'w_up', 'w_down', 'ws_gate', 'ws_up', 'ws_down')}
    del _L0_ffn_all
    return {'x': x, 'ctx_1024': ctx_1024, 'g_xattn': g_xattn, 'g_ffn': g_ffn, 'L0_xattn_Wq': _L0_xattn_in['Wq'], 'L0_xattn_Wk': _L0_xattn_in['Wk'], 'L0_xattn_Wv': _L0_xattn_in['Wv'], 'L0_xattn_Wo': _L0_xattn_in['Wo'], 'L0_xattn_bo': _L0_xattn_in['bo'], 'L0_ffn_router_w': _L0_ffn_in['router_w'], 'L0_ffn_w_gate': _L0_ffn_in['w_gate'], 'L0_ffn_w_up': _L0_ffn_in['w_up'], 'L0_ffn_w_down': _L0_ffn_in['w_down'], 'L0_ffn_ws_gate': _L0_ffn_in['ws_gate'], 'L0_ffn_ws_up': _L0_ffn_in['ws_up'], 'L0_ffn_ws_down': _L0_ffn_in['ws_down']}

def reference(x, ctx_1024, g_xattn, g_ffn, L0_xattn_Wq, L0_xattn_Wk, L0_xattn_Wv, L0_xattn_Wo, L0_xattn_bo, L0_ffn_router_w, L0_ffn_w_gate, L0_ffn_w_up, L0_ffn_w_down, L0_ffn_ws_gate, L0_ffn_ws_up, L0_ffn_ws_down):
    import jax
    import jax.numpy as jnp

    def _L0_xattn_ref(x, context, Wq, Wk, Wv, Wo, bo):
        import jax, jax.numpy as jnp
        import numpy as np
        HIDDEN = 512
        HEADS = 16
        HEAD_DIM = HIDDEN // HEADS
        SCALE = 1.0 / np.sqrt(HEAD_DIM).astype(np.float32)
        b, t, c = x.shape
        kv_t = context.shape[1]
        q = x @ Wq.T
        k = context @ Wk.T
        v = context @ Wv.T
        q = q.reshape(b, t, HEADS, HEAD_DIM).transpose(0, 2, 1, 3)
        k = k.reshape(b, kv_t, HEADS, HEAD_DIM).transpose(0, 2, 1, 3)
        v = v.reshape(b, kv_t, HEADS, HEAD_DIM).transpose(0, 2, 1, 3)
        scores = jnp.einsum('bhqd,bhkd->bhqk', q, k) * SCALE
        causal = jnp.tril(jnp.ones((t, kv_t), dtype=bool))
        scores = jnp.where(causal[None, None, :, :], scores, -jnp.inf)
        probs = jax.nn.softmax(scores, axis=-1)
        y = jnp.einsum('bhqk,bhkd->bhqd', probs, v)
        y = y.transpose(0, 2, 1, 3).reshape(b, t, c)
        return y @ Wo.T + bo

    def _L0_ffn_ref(hidden_states, router_w, w_gate, w_up, w_down, ws_gate, ws_up, ws_down):
        import jax, jax.numpy as jnp
        import numpy as np
        TOP_K = 6

        def _glu_mlp(x, wg, wu, wd):
            return jax.nn.silu(x @ wg) * (x @ wu) @ wd
        B, S, D = hidden_states.shape
        x = hidden_states.reshape(-1, D)
        scores = jax.nn.softmax(x @ router_w, axis=-1)
        topk_w, topk_idx = jax.lax.top_k(scores, TOP_K)
        g = jnp.einsum('td,edf->etf', x, w_gate)
        u = jnp.einsum('td,edf->etf', x, w_up)
        f_all = jnp.einsum('etf,efd->ted', jax.nn.silu(g) * u, w_down)
        picked = jnp.take_along_axis(f_all, topk_idx[:, :, None], axis=1)
        y = jnp.sum(picked * topk_w[:, :, None], axis=1).reshape(B, S, D)
        y = y + _glu_mlp(hidden_states, ws_gate, ws_up, ws_down)
        return y
    x = x + jnp.tanh(g_xattn[0]) * _L0_xattn_ref(_layernorm(x, axis=-1), ctx_1024, L0_xattn_Wq, L0_xattn_Wk, L0_xattn_Wv, L0_xattn_Wo, L0_xattn_bo)
    x = x + jnp.tanh(g_ffn[0]) * _L0_ffn_ref(_layernorm(x, axis=-1), L0_ffn_router_w, L0_ffn_w_gate, L0_ffn_w_up, L0_ffn_w_down, L0_ffn_ws_gate, L0_ffn_ws_up, L0_ffn_ws_down)
    return x

_drawn_inputs = setup_inputs


def setup_inputs(seed=0):
    import zlib

    import numpy as np

    out = dict(_drawn_inputs(seed))
    spreads = {'L0_xattn_bo': (0.0, 0.1)}
    factors = {'L0_xattn_Wq': 8.0,
     'L0_xattn_Wk': 8.0,
     'L0_ffn_router_w': 8.0,
     'L0_ffn_w_gate': 4.748,
     'L0_ffn_w_up': 4.656,
     'L0_ffn_w_down': 4.662,
     'L0_ffn_ws_gate': 4.424,
     'L0_ffn_ws_up': 4.35,
     'L0_ffn_ws_down': 4.345}
    for name, (base, spread) in spreads.items():
        noise = np.random.default_rng([zlib.crc32(name.encode()), seed]).standard_normal(out[name].shape)
        drawn = base * np.exp(spread * noise) if base else spread * noise
        out[name] = jnp.asarray(drawn.astype(out[name].dtype))
    for name, factor in factors.items():
        out[name] = (out[name] * factor).astype(out[name].dtype)
    return out
```

```python
from contextlib import ExitStack

import concourse.bass as bass
from concourse import mybir

F32 = mybir.dt.float32
F32R = mybir.dt.float32r
F16 = mybir.dt.float16
BF16 = mybir.dt.bfloat16
I32 = mybir.dt.int32
ALU = mybir.AluOpType
ACT = mybir.ActivationFunctionType
AX = mybir.AxisListType

P = 128
B, S, D = 16, 256, 512
H = 16
DH = D // H
C = D // P
JH = P // DH
T = S // P
SCALE = float(DH) ** -0.5
EPS = 1e-5
E, F, TOP = 8, 256, 6
NE = E + 2
NEG = -3.0e38
HALF_TOKENS = B * S // 2
BLK = 512
NB = HALF_TOKENS // BLK
BT = BLK // P
FC = F // P
RSQRT_MAGIC = float(0x5F3759DF)
DMA = 16


class At:

    def __init__(self, r, step, k):
        self.r, self.step, self.k = r, step, k

    def __add__(self, k):
        return At(self.r, self.step, self.k + k)

    def parity(self):
        return self.k % 2

    def over(self, n):
        return At(self.r, self.step // n, self.k // n)

    def times(self, c, plus=0):
        fixed = c * self.k + plus
        return fixed if isinstance(self.r, int) else self.r * (c * self.step) + fixed


def wait(eng, sem, value):
    if not isinstance(value, int) or value > 0:
        eng.wait_ge(sem, value)


def row(view, index):
    v = index.times(1)
    if isinstance(v, int):
        return view[v]
    names = ["o", "p", "t", "d"][: len(view.shape)]
    rest = " ".join(names[2:])
    return view[bass.ds(v, 1)].rearrange(f"o p {rest} -> (o p) {rest}")


def newton_rsqrt(pool, chain, passed, count, y, hv, a):
    for _ in range(3):
        for out, in0, in1 in ((a, y, y), (a, a, hv), (a, a, None), (y, y, a)):
            if in1 is None:
                pool.sem_inc(passed, 1)
                ins = pool.tensor_scalar(out, in0, 1.5, None, ALU.add)
            else:
                ins = pool.tensor_tensor(out, in0, in1, ALU.mult)
            count[0] += 1
            ins.then_inc(chain, 1)
            pool.wait_ge(chain, count[0] if isinstance(count[1], int) else count[1] + count[0])


def gated_block(nc, x, ctx_t, g_xattn, g_ffn, wq_t, wk_t, wv_t, wo_t, bo, router, w_gate, w_up, w_down, out):
    with ExitStack() as both:
        ident = both.enter_context(nc.sbuf_tensor("ident", [P, P], F32))
        gates = both.enter_context(nc.sbuf_tensor("gates", [P, 2], F32))
        tanh_gates = both.enter_context(nc.sbuf_tensor("tanh_gates", [P, 2], F32))
        x1 = nc.dram_tensor("x1_between", [B * S, D], F32, kind="Internal").ap()
        with ExitStack() as ctx:
            attention(nc, ctx, x, ctx_t, g_xattn, g_ffn, wq_t, wk_t, wv_t, wo_t, bo, x1, ident, gates, tanh_gates)
        with ExitStack() as ctx:
            experts(nc, ctx, x1, router, w_gate, w_up, w_down, out, ident, tanh_gates)


def attention(nc, ctx, x, ctx_t, g_xattn, g_ffn, wq_t, wk_t, wv_t, wo_t, bo, x1, ident, gates, tanh_gates):
    def sb(name, shape, dt=F32):
        return ctx.enter_context(nc.sbuf_tensor(name, shape, dt))

    def sem(name):
        return ctx.enter_context(nc.semaphore(name))

    w_hi, w_lo = (sb(f"w_{n}", [P, 4, C, D], F32R) for n in ("hi", "lo"))
    WQ, WK, WV, WO = range(4)
    q_stack = [sb(f"q_stack{i}", [P, H, S], F32R) for i in range(2)]
    k_stack = [sb(f"k_stack{i}", [P, H, S], F32R) for i in range(2)]
    x_in = sb("x_in", [P, T, D])
    c_in = sb("c_in", [P, C, S])
    c_hi, c_lo = sb("c_hi", [P, C, S], F32R), sb("c_lo", [P, C, S], F32R)
    t_hi, t_lo = sb("t_hi", [P, C, S], F32R), sb("t_lo", [P, C, S], F32R)
    q_hi, q_lo = sb("q_hi", [P, C, S], F32R), sb("q_lo", [P, C, S], F32R)
    k_hi, k_lo = sb("k_hi", [P, C, S], F32R), sb("k_lo", [P, C, S], F32R)
    v_parts = [sb(f"v_parts{i}", [P, T, 3, D], BF16) for i in range(2)]
    v_rest = sb("v_rest", [P, D])
    masked = [sb(f"masked{i}", [P, 3 * P]) for i in range(2)]
    probs = [sb(f"probs{i}", [P, 3 * P]) for i in range(2)]
    pt_hi = [sb(f"pt_hi{i}", [P, 3 * P], F16) for i in range(2)]
    pt_lo = [sb(f"pt_lo{i}", [P, 3 * P], F16) for i in range(2)]
    y = sb("y", [P, T, D])
    y_sum = sb("y_sum", [P, T, JH, DH])
    x_res = sb("x_res", [P, T, D])
    mask = sb("mask", [P, 2 * P])
    bias = sb("bias", [P, D])
    row_max = sb("row_max", [P, H, T])
    neg_max = sb("neg_max", [P, H, T])
    row_sum = sb("row_sum", [P, H, T])
    row_inv = sb("row_inv", [P, JH, T])
    stats, mv = sb("stats", [P, T, 6]), sb("mv", [P, T, 2])
    var_eps, shifted = sb("var_eps", [P, T]), sb("shifted", [P, T], I32)
    half_var, rstd, newton = sb("half_var", [P, T]), sb("rstd", [P, T]), sb("newton", [P, T])

    bank = [ctx.enter_context(nc.psum_tensor(f"bank{i}", [P, D], F32)) for i in range(2)]
    sc_ps = [ctx.enter_context(nc.psum_tensor(f"scores{i}", [P, T, S], F32)) for i in range(2)]
    pt_ps = [ctx.enter_context(nc.psum_tensor(f"probs_t{i}", [P, D], F32)) for i in range(2)]
    y_ps = [ctx.enter_context(nc.psum_tensor(f"y{i}", [P, JH, P], F32)) for i in range(T)]

    raw_loaded = [sem(f"raw_loaded{i}") for i in range(2)]
    small_loaded = sem("small_loaded")
    x_loaded, c_loaded, res_loaded = sem("x_loaded"), sem("c_loaded"), sem("res_loaded")
    stacked = [sem(f"stacked{i}") for i in range(2)]
    x1_stored = sem("x1_stored")
    ident_made, mask_made, bias_made = sem("ident_made"), sem("mask_made"), sem("bias_made")
    pool_chain, xn_made, c_lo_made, v3_made = sem("pool_chain"), sem("xn_made"), sem("c_lo_made"), sem("v3_made")
    neg_made, res_made = sem("neg_made"), sem("res_made")
    pool_passed, dve_passed = sem("pool_passed"), sem("dve_passed")
    w_hi_made, tanh_made, c_hi_made = sem("w_hi_made"), sem("tanh_made"), sem("c_hi_made")
    xt_hi_made, q_hi_made, k_hi_made = sem("xt_hi_made"), sem("q_hi_made"), sem("k_hi_made")
    v1_made, v2_made, yt_hi_made = sem("v1_made"), sem("v2_made"), sem("yt_hi_made")
    probs_made, pt_hi_made = sem("probs_made"), sem("pt_hi_made")
    w_lo_made, guess_made, norm_chain = sem("w_lo_made"), sem("guess_made"), sem("norm_chain")
    group_chain = sem("group_chain")
    xt_lo_made, q_lo_made, k_lo_made = sem("xt_lo_made"), sem("q_lo_made"), sem("k_lo_made")
    v_rest_made, yt_lo_made, x1_made = sem("v_rest_made"), sem("yt_lo_made"), sem("x1_made")
    max_made, pt_lo_made, y_made = sem("max_made"), sem("pt_lo_made"), sem("y_made")
    xt_done, q_done, k_done, v_done = sem("xt_done"), sem("q_done"), sem("k_done"), sem("v_done")
    yt_done, o_done = sem("yt_done"), sem("o_done")
    scores_done, pt_done, pv_done = sem("scores_done"), sem("pt_done"), sem("pv_done")

    x_v = x.rearrange("(b t p) d -> b p t d", p=P, t=T)
    x1_v = x1.rearrange("(b t p) d -> b p t d", p=P, t=T)
    c_v = ctx_t.rearrange("(c p) (b t) -> b p c t", p=P, b=B)
    w_v = [w.rearrange("(c p) o -> p c o", p=P) for w in (wq_t, wk_t, wv_t, wo_t)]
    raw = [x_res, y]
    HC = C // 2
    N_RAW = 4 * 2
    STACK_DMAS = 2 * 3 * JH

    FIRST, PAIRS = 3, 5

    def iterations(eng, run):
        for i in range(-1, FIRST):
            run(At(0, 2, i))
        with eng.Fori(0, PAIRS) as r:
            for u in range(2):
                run(At(r, 2, FIRST + u))
        for i in range(FIRST + 2 * PAIRS, B + 1):
            run(At(0, 2, i))

    def has(i, ahead):
        return not isinstance(i.r, int) or 0 <= i.k + ahead < B

    def lagging(i, s, lag):
        back = s < lag
        if not has(i, -back):
            return None
        return i + (-1 if back else 0), (s - lag) % H

    X_SLOT, Y_SLOT, C_SLOT, LN_SLOT = 0, 5, 2, 8
    Q_SLOTS, K_SLOTS = (1, 2, 3, 4), (6, 7, 8, 9)
    O_SLOTS, V_SLOTS = (10, 11), (13, 15)
    TR_LAG, COPY_LAG, PV_LAG = 1, 2, 3
    GROUP_SLOT = PV_LAG + JH - 1

    with nc.Block() as block:
        @block.sync
        def _(sp):
            sp.dma_start(gates[:, 0:1], g_xattn.partition_broadcast(P)).then_inc(small_loaded, DMA)
            sp.dma_start(gates[:, 1:2], g_ffn.partition_broadcast(P)).then_inc(small_loaded, DMA)
            sp.dma_start(bias[:], bo.partition_broadcast(P)).then_inc(small_loaded, DMA)
            sp.dma_start(x_in[:], x_v[0]).then_inc(x_loaded, DMA)
            sp.dma_start(c_in[:], c_v[0]).then_inc(c_loaded, DMA)
            for n in range(N_RAW):
                wait(sp, w_lo_made, n - 1)
                src = w_v[n // 2][:, (n % 2) * HC:(n % 2 + 1) * HC, :]
                sp.dma_start(raw[n % 2][:], src).then_inc(raw_loaded[n % 2], DMA)

            def stack(dst, j, group, src):
                lo, hi = group * DH, (group + 1) * DH
                return sp.dma_start(dst[lo:hi, j:H:JH, :].bitcast(F32), src[j * DH:(j + 1) * DH].bitcast(F32))

            def run(i):
                n, o, ln = i + 1, i + -1, i + 2
                if has(i, -1):
                    wait(sp, x1_stored, o.times(DMA))
                    sp.dma_start(x_res[:], row(x_v, o)).then_inc(res_loaded, DMA)
                if has(i, 2):
                    sp.wait_ge(xt_done, ln.times(T))
                    sp.dma_start(x_in[:], row(x_v, ln)).then_inc(x_loaded, DMA)
                    sp.wait_ge(c_hi_made, ln.times(1))
                    sp.wait_ge(c_lo_made, ln.times(1))
                    sp.dma_start(c_in[:], row(c_v, ln)).then_inc(c_loaded, DMA)
                if has(i, 1):
                    par = n.parity()
                    wait(sp, scores_done, n.times(H, -H))
                    sp.wait_ge(q_hi_made, n.times(2, 2))
                    sp.wait_ge(q_lo_made, n.times(2, 2))
                    for j in range(JH):
                        stack(q_stack[par], j, 0, q_hi).then_inc(stacked[par], DMA)
                        stack(q_stack[par], j, 1, q_lo).then_inc(stacked[par], DMA)
                        stack(q_stack[par], j, 2, q_hi).then_inc(stacked[par], DMA)
                    sp.wait_ge(k_hi_made, n.times(2, 2))
                    sp.wait_ge(k_lo_made, n.times(2, 2))
                    for j in range(JH):
                        stack(k_stack[par], j, 0, k_hi).then_inc(stacked[par], DMA)
                        stack(k_stack[par], j, 1, k_hi).then_inc(stacked[par], DMA)
                        stack(k_stack[par], j, 2, k_lo).then_inc(stacked[par], DMA)
                if has(i, -1):
                    sp.wait_ge(x1_made, o.times(T, T))
                    sp.dma_start(row(x1_v, o), x_res[:]).then_inc(x1_stored, DMA)

            sp.wait_ge(w_lo_made, N_RAW)
            iterations(sp, run)
            sp.wait_ge(x1_stored, B * DMA)

        @block.gpsimd
        def _(pool):
            pool.memset(ident[:], 0.0).then_inc(pool_chain, 1)
            pool.memset(mask[:], 0.0).then_inc(pool_chain, 1)
            pool.wait_ge(pool_chain, 2)
            pool.affine_select(out=ident[:], in_=ident[:], compare_op=ALU.not_equal, fill=1.0, base=0,
                               pattern=[[-1, P]], channel_multiplier=1).then_inc(ident_made, 1)
            pool.affine_select(out=mask[:, P:], in_=mask[:, P:], compare_op=ALU.is_ge, fill=NEG, base=0,
                               pattern=[[-1, P]], channel_multiplier=1).then_inc(mask_made, 1)
            pool.wait_ge(small_loaded, 3 * DMA)
            pool.wait_ge(tanh_made, 1)
            pool.tensor_scalar(bias[:], bias[:], tanh_gates[:, 0:1], None, ALU.mult).then_inc(bias_made, 1)
            pool.wait_ge(bias_made, 1)

            NEWTON = 12

            def normalise(ln):
                pool.wait_ge(guess_made, ln.times(1, 1))
                first = 2 + NEWTON * ln.k
                base = 0 if isinstance(ln.r, int) else ln.r * (NEWTON * ln.step)
                newton_rsqrt(pool, pool_chain, pool_passed, [first, base], rstd[:], half_var[:], newton[:])
                for t in range(T):
                    pool.sem_inc(pool_passed, 1)
                    pool.tensor_scalar(x_in[:, t, :], x_in[:, t, :], mv[:, t, 0:1], rstd[:, t:t + 1],
                                       ALU.subtract, ALU.mult).then_inc(xn_made, 1)

            def run(i):
                n, o, ln = i + 1, i + -1, i + 2
                for s in range(H):
                    if has(i, 0):
                        pool.wait_ge(max_made, i.times(H, s + 1))
                        pool.sem_inc(pool_passed, 1)
                        pool.tensor_scalar(neg_max[:, s, :], row_max[:, s, :], -SCALE, None,
                                           ALU.mult).then_inc(neg_made, 1)
                    if s == C_SLOT and has(i, 1):
                        pool.wait_ge(c_hi_made, n.times(1, 1))
                        wait(pool, v_done, n.times(T))
                        pool.tensor_tensor(c_lo[:], c_in[:], c_hi[:].bitcast(F32),
                                           ALU.subtract).then_inc(c_lo_made, 1)
                    if s == Y_SLOT and has(i, -1):
                        pool.wait_ge(res_loaded, o.times(DMA, DMA))
                        for t in range(T):
                            pool.tensor_tensor(x_res[:, t, :], x_res[:, t, :], bias[:], ALU.add).then_inc(res_made, 1)
                    if s == LN_SLOT and has(i, 2):
                        normalise(ln)
                    if s in V_SLOTS and has(i, 1):
                        t = V_SLOTS.index(s)
                        pool.wait_ge(v2_made, n.times(T, t + 1))
                        pool.tensor_tensor(v_parts[n.parity()][:, t, 2, :], v_rest[:], v_parts[n.parity()][:, t, 1, :],
                                           ALU.subtract).then_inc(v3_made, 1)

            normalise(At(0, 2, 0))
            iterations(pool, run)

        @block.scalar
        def _(act):
            act.wait_ge(small_loaded, 3 * DMA)
            act.activation(tanh_gates[:], gates[:], ACT.Tanh).then_inc(tanh_made, 1)
            for n in range(N_RAW):
                act.wait_ge(raw_loaded[n % 2], (n // 2 + 1) * DMA)
                act.copy(w_hi[:, n // 2, (n % 2) * HC:(n % 2 + 1) * HC, :], raw[n % 2][:]).then_inc(w_hi_made, 1)

            def run(i):
                n, o = i + 1, i + -1
                for s in range(H):
                    if (bh := lagging(i, s, COPY_LAG)):
                        b, h = bh
                        act.wait_ge(pt_done, b.times(H, h + 1))
                        wait(act, pv_done, b.times(H, h - 1))
                        act.copy(pt_hi[h % 2][:], pt_ps[h % 2][:, 0:3 * P]).then_inc(pt_hi_made, 1)
                    if has(i, 0):
                        act.wait_ge(neg_made, i.times(H, s + 1))
                        wait(act, pt_done, i.times(H, s - 1))
                        act.activation(probs[s % 2][:, 0:P], masked[s % 2][:, 0:P], ACT.Exp, bias=neg_max[:, s, 0:1],
                                       scale=SCALE, accum_out=row_sum[:, s, 0:1])
                        act.activation(probs[s % 2][:, P:], masked[s % 2][:, P:], ACT.Exp, bias=neg_max[:, s, 1:2],
                                       scale=SCALE, accum_out=row_sum[:, s, 1:2]).then_inc(probs_made, 1)
                    if has(i, 1):
                        if s == X_SLOT:
                            for t in range(T):
                                act.wait_ge(xt_done, n.times(T, t + 1))
                                if t == 0:
                                    wait(act, q_done, n.times(2))
                                    wait(act, o_done, n.times(T, -2 * T))
                                act.copy(t_hi[:, :, t * P:(t + 1) * P],
                                         bank[t][:].rearrange("p (c t) -> p c t", c=C)).then_inc(xt_hi_made, 1)
                        if s == C_SLOT:
                            act.wait_ge(c_loaded, n.times(DMA, DMA))
                            wait(act, v_done, n.times(T))
                            act.copy(c_hi[:], c_in[:]).then_inc(c_hi_made, 1)
                        for slots, hi, done, made in ((Q_SLOTS, q_hi, q_done, q_hi_made), (K_SLOTS, k_hi, k_done, k_hi_made)):
                            if s in slots[1::2]:
                                u = slots.index(s) // 2
                                act.wait_ge(done, n.times(2, u + 1))
                                if u == 0 and (not isinstance(n.r, int) or n.k > 0):
                                    m = n + -1
                                    act.wait_ge(stacked[m.parity()], m.over(2).times(STACK_DMAS * DMA, STACK_DMAS * DMA))
                                act.copy(hi[:, 2 * u:2 * u + 2, :],
                                         bank[u][:].rearrange("p (m t) -> p m t", m=2)).then_inc(made, 1)
                        if s in V_SLOTS:
                            t, parts = V_SLOTS.index(s), v_parts[n.parity()]
                            act.wait_ge(v_done, n.times(T, t + 1))
                            if t == 0:
                                wait(act, pv_done, n.times(H, -H))
                            act.copy(parts[:, t, 0, :], bank[t][:]).then_inc(v1_made, 1)
                            act.wait_ge(v_rest_made, n.times(T, t + 1))
                            act.copy(parts[:, t, 1, :], v_rest[:]).then_inc(v2_made, 1)
                    if s == Y_SLOT and has(i, -1):
                        for t in range(T):
                            act.wait_ge(yt_done, o.times(T, t + 1))
                            if t == 0 and has(i, 1):
                                act.wait_ge(q_done, n.times(2, 2))
                            elif t == 0:
                                wait(act, o_done, o.times(T))
                            act.copy(t_hi[:, :, t * P:(t + 1) * P],
                                     bank[t][:].rearrange("p (c t) -> p c t", c=C)).then_inc(yt_hi_made, 1)

            iterations(act, run)

        @block.vector
        def _(dve):
            NORM_STEPS = 2 * T + 2
            PER_GROUP = T + 1

            def statistics(ln):
                dve.wait_ge(x_loaded, ln.times(DMA, DMA))
                for t in range(T):
                    dve.bn_stats(stats[:, t, :], x_in[:, t, :]).then_inc(norm_chain, 1)
                dve.wait_ge(norm_chain, ln.times(NORM_STEPS, T))
                wait(dve, xn_made, ln.times(T))
                dve.sem_inc(dve_passed, 1)
                for t in range(T):
                    dve.bn_aggr(mv[:, t, :], stats[:, t, :]).then_inc(norm_chain, 1)
                dve.wait_ge(norm_chain, ln.times(NORM_STEPS, 2 * T))
                dve.tensor_scalar(var_eps[:], mv[:, :, 1], EPS, None, ALU.add).then_inc(norm_chain, 1)
                dve.wait_ge(norm_chain, ln.times(NORM_STEPS, 2 * T + 1))
                dve.tensor_scalar(shifted[:], var_eps[:].bitcast(I32), 1, None,
                                  ALU.logical_shift_right).then_inc(norm_chain, 1)
                dve.tensor_scalar(half_var[:], var_eps[:], -0.5, None, ALU.mult)
                dve.wait_ge(norm_chain, ln.times(NORM_STEPS, 2 * T + 2))
                dve.tensor_scalar(rstd[:].bitcast(I32), shifted[:], -1.0, RSQRT_MAGIC, ALU.mult,
                                  ALU.add).then_inc(guess_made, 1)

            for n in range(N_RAW):
                dve.wait_ge(w_hi_made, n + 1)
                half = slice((n % 2) * HC, (n % 2 + 1) * HC)
                dve.tensor_tensor(w_lo[:, n // 2, half, :], raw[n % 2][:], w_hi[:, n // 2, half, :].bitcast(F32),
                                  ALU.subtract).then_inc(w_lo_made, 1)
                if n == 1:
                    statistics(At(0, 2, 0))

            def close_group(b, g):
                steps = PER_GROUP * (H // JH)
                first, heads = PER_GROUP * g, slice(JH * g, JH * (g + 1))
                dve.wait_ge(pv_done, b.times(H, JH * (g + 1)))
                if g == 0:
                    wait(dve, yt_done, b.times(T))
                    if isinstance(b.r, int) and b.k == 0:
                        dve.wait_ge(w_lo_made, N_RAW)
                dve.reciprocal(row_inv[:], row_sum[:, heads, :]).then_inc(group_chain, 1)
                for t in range(T):
                    dve.tensor_reduce(y_sum[:, t], y_ps[t][:, :, 0:3 * DH].rearrange("p h (x d) -> p h d x", x=3),
                                      AX.X, ALU.add).then_inc(group_chain, 1)
                dve.wait_ge(group_chain, b.times(steps, first + PER_GROUP))
                for t in range(T):
                    dve.tensor_tensor(y[:, t, JH * DH * g:JH * DH * (g + 1)].rearrange("p (h d) -> p h d", d=DH), y_sum[:, t],
                                      row_inv[:, :, t:t + 1].to_broadcast([P, JH, DH]), ALU.mult).then_inc(y_made, 1)

            dve.wait_ge(mask_made, 1)

            def run(i):
                n, o, ln = i + 1, i + -1, i + 2
                for s in range(H):
                    if has(i, 0):
                        dve.wait_ge(scores_done, i.times(H, s + 1))
                        wait(dve, probs_made, i.times(H, s - 1))
                        dve.sem_inc(dve_passed, 1)
                        for t in range(T):
                            keys = slice(0, P * (t + 1))
                            dst = masked[s % 2][:, 0:P] if t == 0 else masked[s % 2][:, P:]
                            ins = dve.tensor_tensor_reduce(dst, sc_ps[s % 2][:, t, keys], mask[:, P * (1 - t):], 1.0, NEG,
                                                           ALU.add, ALU.max, row_max[:, s, t:t + 1])
                        ins.then_inc(max_made, 1)
                    if (bh := lagging(i, s, COPY_LAG)):
                        b, h = bh
                        dve.wait_ge(pt_hi_made, b.times(H, h + 1))
                        dve.tensor_tensor(pt_lo[h % 2][:], pt_ps[h % 2][:, 0:3 * P], pt_hi[h % 2][:],
                                          ALU.subtract).then_inc(pt_lo_made, 1)
                    if has(i, 1):
                        if s == X_SLOT:
                            for t in range(T):
                                dve.wait_ge(xt_hi_made, n.times(T, t + 1))
                                part = slice(t * P, (t + 1) * P)
                                dve.tensor_tensor(t_lo[:, :, part], bank[t][:].rearrange("p (c t) -> p c t", c=C),
                                                  t_hi[:, :, part].bitcast(F32), ALU.subtract).then_inc(xt_lo_made, 1)
                        for slots, hi, lo, hi_made, made in ((Q_SLOTS, q_hi, q_lo, q_hi_made, q_lo_made),
                                                             (K_SLOTS, k_hi, k_lo, k_hi_made, k_lo_made)):
                            if s in slots[1::2]:
                                u = slots.index(s) // 2
                                part = slice(2 * u, 2 * u + 2)
                                dve.wait_ge(hi_made, n.times(2, u + 1))
                                dve.tensor_tensor(lo[:, part, :], bank[u][:].rearrange("p (m t) -> p m t", m=2),
                                                  hi[:, part, :].bitcast(F32), ALU.subtract).then_inc(made, 1)
                        if s in V_SLOTS:
                            t = V_SLOTS.index(s)
                            dve.wait_ge(v1_made, n.times(T, t + 1))
                            wait(dve, v3_made, n.times(T, t))
                            dve.tensor_tensor(v_rest[:], bank[t][:], v_parts[n.parity()][:, t, 0, :],
                                              ALU.subtract).then_inc(v_rest_made, 1)
                    if has(i, -1):
                        if s == Y_SLOT:
                            for t in range(T):
                                dve.wait_ge(yt_hi_made, o.times(T, t + 1))
                                part = slice(t * P, (t + 1) * P)
                                dve.tensor_tensor(t_lo[:, :, part], bank[t][:].rearrange("p (c t) -> p c t", c=C),
                                                  t_hi[:, :, part].bitcast(F32), ALU.subtract).then_inc(yt_lo_made, 1)
                        if s in O_SLOTS:
                            t = O_SLOTS.index(s)
                            dve.wait_ge(o_done, o.times(T, t + 1))
                            dve.wait_ge(res_made, o.times(T, t + 1))
                            dve.scalar_tensor_tensor(out=x_res[:, t, :], in0=bank[t][:], scalar=tanh_gates[:, 0:1],
                                                     in1=x_res[:, t, :], op0=ALU.mult, op1=ALU.add).then_inc(x1_made, 1)
                    if s == LN_SLOT and has(i, 2):
                        statistics(ln)
                    if (bh := lagging(i, s, GROUP_SLOT)) and bh[1] % JH == 0:
                        close_group(bh[0], bh[1] // JH)

            iterations(dve, run)

        @block.tensor
        def _(pe):
            pe.wait_ge(ident_made, 1)

            def transpose_rows(src, t, dst):
                for c in range(C):
                    ins = pe.transpose(dst[:, c * P:(c + 1) * P], src[:, t, c * P:(c + 1) * P], ident[:])
                return ins

            def three_pass(dst, stationary, moving):
                k = 0
                for c in range(C):
                    for a, b in ((0, 0), (1, 0), (0, 1)):
                        ins = pe.matmul(dst, stationary[a](c), moving[b](c), start=(k == 0), stop=(k == 3 * C - 1))
                        k += 1
                return ins

            def weight(part, mat, lo=0, hi=D):
                return lambda c: part[:, mat, c, lo:hi]

            def run(i):
                n, o = i + 1, i + -1
                fixed = isinstance(i.r, int)
                for s in range(H):
                    if has(i, 0):
                        par = i.parity()
                        if s == 0:
                            pe.wait_ge(stacked[par], i.over(2).times(STACK_DMAS * DMA, STACK_DMAS * DMA))
                        wait(pe, max_made, i.times(H, s - 1))
                        rows = slice(0, 3 * DH)
                        for t in range(T):
                            ins = pe.matmul(sc_ps[s % 2][:, t, :], q_stack[par][rows, s, t * P:(t + 1) * P],
                                            k_stack[par][rows, s, :], start=True, stop=True)
                        ins.then_inc(scores_done, 1)
                    if (bh := lagging(i, s, PV_LAG)):
                        b, h = bh
                        g, hg, v = h // JH, h % JH, v_parts[b.parity()]
                        if h == 0:
                            pe.wait_ge(v3_made, b.times(T, T))
                        if hg == 0:
                            wait(pe, y_made, b.times(T * H // JH, T * g))
                        pe.wait_ge(pt_hi_made, b.times(H, h + 1))
                        pe.wait_ge(pt_lo_made, b.times(H, h + 1))
                        col = slice(h * DH, (h + 1) * DH)
                        for t, blocks in ((0, ((0, 0),)), (1, ((1, 0), (2, 1)))):
                            for k, (blk, key) in enumerate(blocks):
                                at, last = slice(blk * P, (blk + 1) * P), k == len(blocks) - 1
                                dst = y_ps[t][:, hg, 0:3 * DH].rearrange("p (x d) -> p x d", d=DH)
                                pe.matmul(dst, pt_hi[h % 2][:, at], v[:, key, 0:3, col],
                                          start=(k == 0), stop=False)
                                ins = pe.matmul(dst[:, 0:2], pt_lo[h % 2][:, at], v[:, key, 0:2, col],
                                                start=False, stop=last)
                        ins.then_inc(pv_done, 1)
                    if has(i, 1):
                        if s == X_SLOT:
                            for t in range(T):
                                pe.wait_ge(xn_made, n.times(T, t + 1))
                                if not fixed or n.k > 0:
                                    pe.wait_ge(v_rest_made, n.times(T, t + 1 - T))
                                transpose_rows(x_in, t, bank[t]).then_inc(xt_done, 1)
                        if s in Q_SLOTS:
                            m = Q_SLOTS.index(s)
                            if m == 0:
                                pe.wait_ge(xt_hi_made, n.times(T, T))
                                pe.wait_ge(xt_lo_made, n.times(T, T))
                                wait(pe, w_lo_made, 2 if fixed and n.k == 0 else 0)
                            lo, hi = m * P, (m + 1) * P
                            ins = three_pass(bank[m // 2][:, (m % 2) * S:(m % 2 + 1) * S],
                                             (weight(w_hi, WQ, lo, hi), weight(w_lo, WQ, lo, hi)),
                                             (lambda c: t_hi[:, c, :], lambda c: t_lo[:, c, :]))
                            if m % 2:
                                ins.then_inc(q_done, 1)
                        if s in K_SLOTS:
                            m = K_SLOTS.index(s)
                            if m == 0:
                                pe.wait_ge(c_hi_made, n.times(1, 1))
                                pe.wait_ge(c_lo_made, n.times(1, 1))
                                wait(pe, w_lo_made, 4 if fixed and n.k == 0 else 0)
                            if m % 2 == 0 and has(i, -1):
                                pe.wait_ge(yt_lo_made, o.times(T, m // 2 + 1))
                            elif m % 2 == 0:
                                pe.wait_ge(q_lo_made, n.times(2, m // 2 + 1))
                            lo, hi = m * P, (m + 1) * P
                            ins = three_pass(bank[m // 2][:, (m % 2) * S:(m % 2 + 1) * S],
                                             (weight(w_hi, WK, lo, hi), weight(w_lo, WK, lo, hi)),
                                             (lambda c: c_hi[:, c, :], lambda c: c_lo[:, c, :]))
                            if m % 2:
                                ins.then_inc(k_done, 1)
                        if s in V_SLOTS:
                            t = V_SLOTS.index(s)
                            if has(i, -1):
                                pe.wait_ge(x1_made, o.times(T, t + 1))
                            else:
                                pe.wait_ge(k_lo_made, n.times(2, t + 1))
                            wait(pe, w_lo_made, N_RAW if fixed and n.k == 0 else 0)
                            part = slice(t * P, (t + 1) * P)
                            three_pass(bank[t][:], (lambda c: c_hi[:, c, part], lambda c: c_lo[:, c, part]),
                                       (weight(w_hi, WV), weight(w_lo, WV))).then_inc(v_done, 1)
                    if has(i, -1):
                        if s == Y_SLOT:
                            pe.wait_ge(y_made, o.times(T * H // JH, T * H // JH))
                            for t in range(T):
                                if has(i, 1):
                                    pe.wait_ge(q_lo_made, n.times(2, t + 1))
                                else:
                                    wait(pe, x1_made, o.times(T, t + 1 - T))
                                    wait(pe, v_rest_made, B * T)
                                transpose_rows(y, t, bank[t]).then_inc(yt_done, 1)
                        if s in O_SLOTS:
                            t = O_SLOTS.index(s)
                            if t == 0:
                                pe.wait_ge(yt_hi_made, o.times(T, T))
                                pe.wait_ge(yt_lo_made, o.times(T, T))
                            if has(i, 1):
                                pe.wait_ge(k_lo_made, n.times(2, t + 1))
                            part = slice(t * P, (t + 1) * P)
                            three_pass(bank[t][:], (lambda c: t_hi[:, c, part], lambda c: t_lo[:, c, part]),
                                       (weight(w_hi, WO), weight(w_lo, WO))).then_inc(o_done, 1)
                    if (bh := lagging(i, s, TR_LAG)):
                        b, h = bh
                        pe.wait_ge(probs_made, b.times(H, h + 1))
                        wait(pe, pt_lo_made, b.times(H, h - 1))
                        for k in range(3):
                            ins = pe.transpose(pt_ps[h % 2][:, k * P:(k + 1) * P], probs[h % 2][:, k * P:(k + 1) * P], ident[:])
                        ins.then_inc(pt_done, 1)

            iterations(pe, run)


def experts(nc, ctx, x1, router, w_gate, w_up, w_down, out, ident, tanh_gates):
    def sb(name, shape, dt=F32):
        return ctx.enter_context(nc.sbuf_tensor(name, shape, dt))

    def sem(name):
        return ctx.enter_context(nc.semaphore(name))

    HALVES, U = 2, 2
    STEPS = NE * NB
    TURN = U * NB
    WP = C * F
    GATE, UP, DOWN = range(3)

    xt_hi, xt_lo = sb("xt_hi", [P, NB, C, BLK], F32R), sb("xt_lo", [P, NB, C, BLK], F32R)
    SLOTS = NB + 1
    acc = sb("acc", [P, SLOTS, BT, D])
    w_raw = sb("w_raw", [P, 3, WP])
    e_hi = [sb(f"e_hi{i}", [P, 3, WP], F32R) for i in range(2)]
    e_lo = [sb(f"e_lo{i}", [P, 3, WP], F32R) for i in range(2)]
    h_hi = [sb(f"h_hi{i}", [P, FC, BLK], F32R) for i in range(2)]
    h_lo = [sb(f"h_lo{i}", [P, FC, BLK], F32R) for i in range(2)]
    silu = [sb(f"silu{i}", [P, BLK]) for i in range(FC)]
    h = [sb(f"h{i}", [P, BLK]) for i in range(FC)]
    xn = [sb(f"xn{i}", [P, D]) for i in range(2)]
    r_raw = sb("r_raw", [P, C, P])
    r_hi, r_lo = sb("r_hi", [P, C, P], F32R), sb("r_lo", [P, C, P], F32R)
    logits_t = sb("logits_t", [P, BLK])
    before = sb("before", [P, E, E])
    stats, mv = sb("norm_stats", [P, BT, 6]), sb("norm_mv", [P, BT, 2])
    var_eps, shifted = sb("norm_var_eps", [P, BT]), sb("norm_shifted", [P, BT], I32)
    half_var, rstd, newton = sb("norm_half_var", [P, BT]), sb("norm_rstd", [P, BT]), sb("norm_newton", [P, BT])
    top, total, inverse = sb("top", [P, BT]), sb("total", [P, BT]), sb("inverse", [P, BT])
    shift, weights, share = sb("shift", [P, BT, E]), sb("weights", [P, BT, E]), sb("share", [P, BT, E])
    rank = sb("rank", [P, BT, E])
    ahead, equal = sb("ahead", [P, BT, E, E]), sb("equal", [P, BT, E, E])
    scale = sb("scale", [P, HALVES * NB, BT, NE])

    gu_ps = [ctx.enter_context(nc.psum_tensor(f"gate_up{i}", [P, 2, BLK], F32)) for i in range(FC)]
    dn_ps = [ctx.enter_context(nc.psum_tensor(f"down{i}", [P, D], F32)) for i in range(BT)]

    raw_loaded = [sem(f"e_raw_loaded{i}") for i in range(3)]
    r_loaded = sem("r_loaded")
    x1_loaded = [sem(f"x1_loaded{i}") for i in range(HALVES * NB)]
    stored = sem("stored")
    e_pool_passed = sem("e_pool_passed")
    r_zeroed, before_made, e_pool_chain, e_xn_made = sem("r_zeroed"), sem("before_made"), sem("e_pool_chain"), sem("e_xn_made")
    silu_made, h_hi_made, e_hi_made = sem("silu_made"), sem("h_hi_made"), sem("e_hi_made")
    r_hi_made, e_xt_hi_made, logits_made, exp_made = sem("r_hi_made"), sem("e_xt_hi_made"), sem("logits_made"), sem("exp_made")
    h_made, h_lo_made, e_lo_made, added = sem("h_made"), sem("h_lo_made"), sem("e_lo_made"), sem("added")
    r_lo_made, e_guess_made, e_xt_lo_made = sem("r_lo_made"), sem("e_guess_made"), sem("e_xt_lo_made")
    shift_made, scale_made = sem("shift_made"), sem("scale_made")
    e_norm_chain, route_chain, shared_set = sem("e_norm_chain"), sem("route_chain"), sem("shared_set")
    gate_done, up_done, down_done = sem("gate_done"), sem("up_done"), sem("down_done")
    e_xt_done, logits_done, logits_back = sem("e_xt_done"), sem("logits_done"), sem("logits_back")

    x1_v = x1.rearrange("(k t p) d -> k p t d", p=P, t=BT)
    out_v = out.rearrange("(k t p) d -> k p t d", p=P, t=BT)
    g_v = w_gate.rearrange("e (c p) f -> e p c f", p=P)
    u_v = w_up.rearrange("e (c p) f -> e p c f", p=P)
    d_v = w_down.rearrange("e (f p) d -> e p f d", p=P)

    def piece(tile, which):
        part = tile[:, which, :]
        return part.rearrange("p (c f) -> p c f", c=FC if which == DOWN else C)

    def slot(k):
        return k % SLOTS

    def steps(eng, run, ready_last=lambda k: None):
        for half in range(HALVES):
            first, last = half * STEPS, (half + 1) * STEPS - TURN
            if half == 0:
                for n in range(TURN):
                    run(At(0, TURN, n), half)
                first += TURN
            with eng.Fori(0, (last - first) // TURN) as r:
                for k in range(TURN):
                    run(At(r, TURN, first + k), half)
            for n in range(last, last + TURN):
                run(At(0, TURN, n), half)
            if half + 1 < HALVES:
                ready_last((half + 2) * NB - 1)

    def follows(n):
        return not isinstance(n.r, int) or n.k < HALVES * STEPS - 1

    def readied(n, half):
        k = n.k - (half + 1) * STEPS
        return half * NB + NB + k + NB - 1 if isinstance(n.r, int) and half + 1 < HALVES and 1 - NB <= k < 0 else None

    with nc.Block() as block:
        @block.sync
        def _(sp):
            sp.wait_ge(r_zeroed, 1)
            sp.dma_start(r_raw[:, :, 0:E], router.rearrange("(c p) e -> p c e", p=P)).then_inc(r_loaded, DMA)

            def load_x1(k):
                sp.dma_start(acc[:, slot(k)], x1_v[k]).then_inc(x1_loaded[k], DMA)

            def load_raw(which, index):
                src = (g_v, u_v, d_v)[which]
                e = index if isinstance(index, int) else bass.ds(index, 1)
                src = src[e] if isinstance(index, int) else src[e].rearrange("o p c f -> (o p) c f")
                sp.dma_start(piece(w_raw, which), src).then_inc(raw_loaded[which], DMA)

            load_x1(0)
            for which in range(3):
                load_raw(which, 0)
            for k in range(1, NB):
                load_x1(k)
            for which in range(3):
                sp.wait_ge(e_lo_made, which + 1)
                load_raw(which, 1)
            load_x1(NB)

            def run(n, half):
                fixed, e, blk = isinstance(n.r, int), n.over(NB), n.k % NB
                if blk < 3 and (not fixed or e.k + 2 < HALVES * NE):
                    sp.wait_ge(e_lo_made, e.times(3, 3 + blk + 1))
                    within = At(e.r, e.step, e.k + 2 - half * NE).times(1)
                    load_raw(blk, within % NE if isinstance(within, int) else within)
                if fixed and n.k % STEPS >= STEPS - NB:
                    k = half * NB + blk
                    sp.wait_ge(added, BT * (n.k + 1))
                    sp.dma_start(out_v[k], acc[:, slot(k)]).then_inc(stored, DMA)
                    if half + 1 < HALVES and blk + 1 < NB:
                        sp.wait_ge(stored, DMA * (blk + 1))
                        load_x1(NB + blk + 1)

            steps(sp, run)
            sp.wait_ge(stored, HALVES * NB * DMA)

        @block.gpsimd
        def _(pool):
            pool.memset(r_raw[:], 0.0).then_inc(r_zeroed, 1)
            pool.memset(before[:], 1.0).then_inc(e_pool_chain, 1)
            pool.wait_ge(e_pool_chain, 1)
            pool.affine_select(out=before[:], in_=before[:], compare_op=ALU.is_gt, fill=0.0, base=0,
                               pattern=[[1, E], [-1, E]], channel_multiplier=0).then_inc(before_made, 1)

            def normalise(k):
                pool.wait_ge(e_guess_made, k + 1)
                newton_rsqrt(pool, e_pool_chain, e_pool_passed, [1 + 12 * k, 0], rstd[:], half_var[:], newton[:])
                for t in range(BT):
                    wait(pool, e_xt_done, BT * k + t - 1)
                    pool.tensor_scalar(xn[t % 2][:], acc[:, slot(k), t, :], mv[:, t, 0:1], rstd[:, t:t + 1],
                                       ALU.subtract, ALU.mult).then_inc(e_xn_made, 1)

            for k in range(HALVES * NB):
                normalise(k)

        @block.scalar
        def _(act):
            def split_hi(e, which):
                act.wait_ge(raw_loaded[which], e.times(DMA, DMA))
                if which != DOWN:
                    wait(act, up_done, e.times(NB * FC, -NB * FC))
                else:
                    wait(act, down_done, e.times(NB * BT, -NB * BT))
                act.copy(e_hi[e.parity()][:, which, :], w_raw[:, which, :]).then_inc(e_hi_made, 1)

            def rows_hi(k):
                for t in range(BT):
                    act.wait_ge(e_xt_done, BT * k + t + 1)
                    if k >= NB and t == 0:
                        act.wait_ge(up_done, FC * (STEPS - NB + k % NB + 1))
                    act.copy(xt_hi[:, k % NB, :, t * P:(t + 1) * P],
                             dn_ps[t][:].rearrange("p (c t) -> p c t", c=C)).then_inc(e_xt_hi_made, 1)

            def copy_logits(k, ps):
                act.wait_ge(logits_done, k + 1)
                act.copy(logits_t[:], ps).then_inc(logits_made, 1)

            def exponentials(k):
                act.wait_ge(shift_made, k + 1)
                act.activation(weights[:], shift[:], ACT.Exp).then_inc(exp_made, 1)

            def hidden(n):
                for f in range(FC):
                    act.wait_ge(gate_done, n.times(FC, f + 1))
                    wait(act, h_made, n.times(FC, f + 1 - FC))
                    act.activation(silu[f][:], gu_ps[f][:, 0, :], ACT.Silu).then_inc(silu_made, 1)
                    act.wait_ge(h_made, n.times(FC, f + 1))
                    wait(act, down_done, n.times(BT, -BT))
                    act.copy(h_hi[n.parity()][:, f, :], h[f][:]).then_inc(h_hi_made, 1)

            def ready(k):
                rows_hi(k)
                copy_logits(k, dn_ps[0][:])
                exponentials(k)

            def run(n, half):
                k = readied(n, half)
                if k is not None:
                    ready(k)
                if follows(n):
                    hidden(n + 1)
                e, blk = n.over(NB) + 1, n.k % NB
                if blk < 3 and (not isinstance(n.r, int) or e.k < HALVES * NE):
                    split_hi(e, blk)

            act.wait_ge(r_loaded, DMA)
            act.copy(r_hi[:], r_raw[:]).then_inc(r_hi_made, 1)
            for which in range(3):
                split_hi(At(0, U, 0), which)
            for k in range(NB):
                rows_hi(k)
                copy_logits(k, gu_ps[0][:, 0, :])
                exponentials(k)
            hidden(At(0, TURN, 0))
            steps(act, run, ready)

        @block.vector
        def _(dve):
            NORM_STEPS, ROUTE_STEPS = 2 * BT + 2, 10

            def split_lo(e, which):
                dve.wait_ge(e_hi_made, e.times(3, which + 1))
                dve.tensor_tensor(e_lo[e.parity()][:, which, :], w_raw[:, which, :],
                                  e_hi[e.parity()][:, which, :].bitcast(F32), ALU.subtract).then_inc(e_lo_made, 1)

            def statistics(k):
                at = NORM_STEPS * k
                dve.wait_ge(x1_loaded[k], DMA)
                for t in range(BT):
                    dve.bn_stats(stats[:, t, :], acc[:, slot(k), t, :]).then_inc(e_norm_chain, 1)
                dve.wait_ge(e_norm_chain, at + BT)
                wait(dve, e_xn_made, BT * k)
                for t in range(BT):
                    dve.bn_aggr(mv[:, t, :], stats[:, t, :]).then_inc(e_norm_chain, 1)
                dve.wait_ge(e_norm_chain, at + 2 * BT)
                dve.tensor_scalar(var_eps[:], mv[:, :, 1], EPS, None, ALU.add).then_inc(e_norm_chain, 1)
                dve.wait_ge(e_norm_chain, at + 2 * BT + 1)
                dve.tensor_scalar(shifted[:], var_eps[:].bitcast(I32), 1, None,
                                  ALU.logical_shift_right).then_inc(e_norm_chain, 1)
                dve.tensor_scalar(half_var[:], var_eps[:], -0.5, None, ALU.mult)
                dve.wait_ge(e_norm_chain, at + 2 * BT + 2)
                dve.tensor_scalar(rstd[:].bitcast(I32), shifted[:], -1.0, RSQRT_MAGIC, ALU.mult,
                                  ALU.add).then_inc(e_guess_made, 1)

            def rows_lo(k):
                for t in range(BT):
                    part = slice(t * P, (t + 1) * P)
                    dve.wait_ge(e_xt_hi_made, BT * k + t + 1)
                    dve.tensor_tensor(xt_lo[:, k % NB, :, part], dn_ps[t][:].rearrange("p (c t) -> p c t", c=C),
                                      xt_hi[:, k % NB, :, part].bitcast(F32), ALU.subtract).then_inc(e_xt_lo_made, 1)

            def route(k, ps):
                count = [ROUTE_STEPS * k]

                def link(ins):
                    count[0] += 1
                    ins.then_inc(route_chain, 1)
                    dve.wait_ge(route_chain, count[0])

                logits = ps.rearrange("p (t e) -> p t e", t=BT)[:, :, 0:E]
                wide, pairs = [P, BT, E], [P, BT, E, E]
                dve.wait_ge(logits_back, k + 1)
                link(dve.tensor_reduce(top[:], logits, AX.X, ALU.max))
                dve.tensor_tensor(shift[:], logits, top[:].unsqueeze(2).to_broadcast(wide),
                                  ALU.subtract).then_inc(shift_made, 1)
                dve.wait_ge(exp_made, k + 1)
                link(dve.tensor_reduce(total[:], weights[:], AX.X, ALU.add))
                link(dve.reciprocal(inverse[:], total[:]))
                link(dve.tensor_tensor(share[:], weights[:], inverse[:].unsqueeze(2).to_broadcast(wide), ALU.mult))
                mine, others = share[:].unsqueeze(3).to_broadcast(pairs), share[:].unsqueeze(2).to_broadcast(pairs)
                link(dve.tensor_tensor(ahead[:], others, mine, ALU.is_gt))
                link(dve.tensor_tensor(equal[:], others, mine, ALU.is_equal))
                link(dve.tensor_tensor(equal[:], equal[:], before[:].unsqueeze(1).to_broadcast(pairs), ALU.mult))
                link(dve.tensor_tensor(ahead[:], ahead[:], equal[:], ALU.add))
                link(dve.tensor_reduce(rank[:], ahead[:], AX.X, ALU.add))
                link(dve.scalar_tensor_tensor(out=rank[:], in0=rank[:], scalar=TOP - 0.5, in1=share[:],
                                              op0=ALU.is_lt, op1=ALU.mult))
                dve.tensor_scalar(scale[:, k, :, 0:E], rank[:], tanh_gates[:, 1:2], None, ALU.mult).then_inc(scale_made, 1)

            def hidden(n):
                for f in range(FC):
                    dve.wait_ge(up_done, n.times(FC, f + 1))
                    dve.wait_ge(silu_made, n.times(FC, f + 1))
                    wait(dve, h_lo_made, n.times(FC, f + 1 - FC))
                    dve.tensor_tensor(h[f][:], gu_ps[f][:, 1, :], silu[f][:], ALU.mult).then_inc(h_made, 1)
                    dve.wait_ge(h_hi_made, n.times(FC, f + 1))
                    dve.tensor_tensor(h_lo[n.parity()][:, f, :], h[f][:], h_hi[n.parity()][:, f, :].bitcast(F32),
                                      ALU.subtract).then_inc(h_lo_made, 1)

            def add(n, half):
                blk = n.k % NB
                e = At(n.r, U, (n.k - half * STEPS) // NB).times(1)
                k = half * NB + blk
                wait(dve, added, n.times(BT))
                for t in range(BT):
                    dve.wait_ge(down_done, n.times(BT, t + 1))
                    share_of = scale[:, k, t, e:e + 1] if isinstance(e, int) else scale[:, k, t, bass.ds(e, 1)]
                    dve.scalar_tensor_tensor(out=acc[:, slot(k), t, :], in0=dn_ps[t][:], scalar=share_of,
                                             in1=acc[:, slot(k), t, :], op0=ALU.mult, op1=ALU.add).then_inc(added, 1)

            def ready_last(k):
                statistics(k)
                rows_lo(k)
                route(k, dn_ps[1][:])

            def run(n, half):
                k = readied(n, half)
                if k is not None:
                    rows_lo(k)
                    route(k, dn_ps[1][:])
                if follows(n):
                    hidden(n + 1)
                add(n, half)
                e, blk = n.over(NB) + 1, n.k % NB
                if blk < 3 and (not isinstance(n.r, int) or e.k < HALVES * NE):
                    split_lo(e, blk)
                following = readied(n + 1, half) if isinstance(n.r, int) else None
                if following is not None:
                    statistics(following)

            for k in range(HALVES * NB):
                ins = dve.tensor_copy(scale[:, k, :, E:], tanh_gates[:, 1:2].unsqueeze(2).to_broadcast([P, BT, NE - E]))
            ins.then_inc(shared_set, 1)
            dve.wait_ge(shared_set, 1)
            dve.wait_ge(before_made, 1)
            statistics(0)
            dve.wait_ge(r_hi_made, 1)
            dve.tensor_tensor(r_lo[:], r_raw[:], r_hi[:].bitcast(F32), ALU.subtract).then_inc(r_lo_made, 1)
            for which in range(3):
                split_lo(At(0, U, 0), which)
            for k in range(NB):
                rows_lo(k)
                if k + 1 < NB:
                    statistics(k + 1)
                route(k, gu_ps[0][:, 1, :])
            hidden(At(0, TURN, 0))
            steps(dve, run, ready_last)

        @block.tensor
        def _(pe):
            def rows(k, ready):
                for t in range(BT):
                    pe.wait_ge(e_xn_made, BT * k + t + 1)
                    if ready:
                        pe.wait_ge(added, ready + t + 1)
                    elif k:
                        pe.wait_ge(e_xt_lo_made, BT * (k - 1) + t + 1)
                    for c in range(C):
                        ins = pe.transpose(dn_ps[t][:, c * P:(c + 1) * P], xn[t % 2][:, c * P:(c + 1) * P], ident[:])
                    ins.then_inc(e_xt_done, 1)

            PASSES = ((0, 0), (1, 0), (0, 1))

            def logits(k, ps, ps_back):
                pe.wait_ge(e_xt_hi_made, BT * (k + 1))
                pe.wait_ge(e_xt_lo_made, BT * (k + 1))
                pe.wait_ge(r_lo_made, 1)
                wait(pe, scale_made, k)
                i = 0
                for c in range(C):
                    for a, b in PASSES:
                        ins = pe.matmul(ps, (r_hi, r_lo)[a][:, c, :], (xt_hi, xt_lo)[b][:, k % NB, c, :],
                                        start=(i == 0), stop=(i == len(PASSES) * C - 1))
                        i += 1
                ins.then_inc(logits_done, 1)
                pe.wait_ge(logits_made, k + 1)
                for t in range(BT):
                    ins = pe.transpose(ps_back[:, t * P:(t + 1) * P], logits_t[:, t * P:(t + 1) * P], ident[:])
                ins.then_inc(logits_back, 1)

            def gate_up(n):
                e, blk = n.over(NB), n.k % NB
                par = e.parity()
                if blk == 0:
                    pe.wait_ge(e_lo_made, e.times(3, 2))
                for f in range(FC):
                    wait(pe, h_made, n.times(FC, f + 1 - FC))
                    for which, done in ((GATE, gate_done), (UP, up_done)):
                        hi, lo = piece(e_hi[par], which), piece(e_lo[par], which)
                        i = 0
                        for c in range(C):
                            for a, b in PASSES:
                                ins = pe.matmul(gu_ps[f][:, which, :], (hi, lo)[a][:, c, f * P:(f + 1) * P],
                                                (xt_hi, xt_lo)[b][:, blk, c, :], start=(i == 0), stop=(i == len(PASSES) * C - 1))
                                i += 1
                        ins.then_inc(done, 1)

            def down(n, free=None):
                e = n.over(NB)
                par, hp = e.parity(), n.parity()
                if n.k % NB == 0:
                    pe.wait_ge(e_lo_made, e.times(3, 3))
                pe.wait_ge(h_hi_made, n.times(FC, FC))
                pe.wait_ge(h_lo_made, n.times(FC, FC))
                hi, lo = piece(e_hi[par], DOWN), piece(e_lo[par], DOWN)
                wait(pe, added, n.times(BT))
                for t in range(BT):
                    if free is not None:
                        pe.wait_ge(e_xt_lo_made, BT * free)
                        pe.wait_ge(scale_made, free)
                    i = 0
                    for f in range(FC):
                        for a, b in PASSES:
                            ins = pe.matmul(dn_ps[t][:], (h_hi, h_lo)[a][hp][:, f, t * P:(t + 1) * P], (hi, lo)[b][:, f, :],
                                            start=(i == 0), stop=(i == len(PASSES) * FC - 1))
                            i += 1
                    ins.then_inc(down_done, 1)

            def ready_last(k):
                rows(k, BT * (STEPS - 1))
                logits(k, dn_ps[0][:], dn_ps[1][:])
                pe.wait_ge(scale_made, k + 1)

            def run(n, half):
                k = readied(n, half)
                if k is not None:
                    rows(k, BT * (n.k - 1))
                    logits(k, dn_ps[0][:], dn_ps[1][:])
                if follows(n):
                    gate_up(n + 1)
                down(n, None if k is None else k + 1)

            for k in range(NB):
                rows(k, 0)
                logits(k, gu_ps[0][:, 0, :], gu_ps[0][:, 1, :])
            pe.wait_ge(scale_made, NB)
            gate_up(At(0, TURN, 0))
            steps(pe, run, ready_last)


def kernel(**inputs):
    import numpy as np
    import concourse.bacc as bacc
    from concourse.bass_utils import run_bass_kernel_spmd

    a = {k: np.asarray(v) for k, v in inputs.items()}
    lay = np.ascontiguousarray

    def with_shared(experts_w, shared, axis):
        parts = np.split(shared, 2, axis=axis)
        return np.concatenate([experts_w, np.stack(parts)])

    arrays = {
        "x": a["x"].reshape(B * S, D),
        "ctx_t": lay(a["ctx_1024"].reshape(B * S, D).T),
        "g_xattn": a["g_xattn"],
        "g_ffn": a["g_ffn"],
        "wq_t": lay(a["L0_xattn_Wq"].T),
        "wk_t": lay(a["L0_xattn_Wk"].T),
        "wv_t": lay(a["L0_xattn_Wv"].T),
        "wo_t": lay(a["L0_xattn_Wo"].T),
        "bo": a["L0_xattn_bo"],
        "router": a["L0_ffn_router_w"],
        "w_gate": with_shared(a["L0_ffn_w_gate"], a["L0_ffn_ws_gate"], 1),
        "w_up": with_shared(a["L0_ffn_w_up"], a["L0_ffn_ws_up"], 1),
        "w_down": with_shared(a["L0_ffn_w_down"], a["L0_ffn_ws_down"], 0),
    }
    nc = bacc.Bacc("TRN2", target_bir_lowering=False, num_devices=1)
    aps = {k: nc.dram_tensor(f"in_{k}", v.shape, mybir.dt.from_np(v.dtype), kind="ExternalInput").ap() for k, v in arrays.items()}
    out = nc.dram_tensor("out_0", (B * S, D), F32, kind="ExternalOutput").ap()
    gated_block(nc, **aps, out=out)
    result = run_bass_kernel_spmd(nc, [{f"in_{k}": v for k, v in arrays.items()}], core_ids=[0])
    return result.results[0]["out_0"].reshape(B, S, D)
```

```python
from contextlib import ExitStack

import concourse.bass as bass
from concourse import mybir

F32 = mybir.dt.float32
F32R = mybir.dt.float32r
F16 = mybir.dt.float16
BF16 = mybir.dt.bfloat16
I32 = mybir.dt.int32
ALU = mybir.AluOpType
ACT = mybir.ActivationFunctionType
AX = mybir.AxisListType

P = 128
B, S, D = 16, 256, 512
H = 16
DH = D // H
C = D // P
JH = P // DH
T = S // P
SCALE = float(DH) ** -0.5
EPS = 1e-5
E, F, TOP = 8, 256, 6
NE = E + 2
NEG = -3.0e38
HALF_TOKENS = B * S // 2
BLK = 512
NB = HALF_TOKENS // BLK
BT = BLK // P
FC = F // P
RSQRT_MAGIC = float(0x5F3759DF)
DMA = 16


class At:

    def __init__(self, r, step, k):
        self.r, self.step, self.k = r, step, k

    def __add__(self, k):
        return At(self.r, self.step, self.k + k)

    def parity(self):
        return self.k % 2

    def over(self, n):
        return At(self.r, self.step // n, self.k // n)

    def times(self, c, plus=0):
        fixed = c * self.k + plus
        return fixed if isinstance(self.r, int) else self.r * (c * self.step) + fixed


def wait(eng, sem, value):
    if not isinstance(value, int) or value > 0:
        eng.wait_ge(sem, value)


def row(view, index):
    v = index.times(1)
    if isinstance(v, int):
        return view[v]
    names = ["o", "p", "t", "d"][: len(view.shape)]
    rest = " ".join(names[2:])
    return view[bass.ds(v, 1)].rearrange(f"o p {rest} -> (o p) {rest}")


def newton_rsqrt(pool, chain, passed, count, y, hv, a, made):
    STEPS = 3
    for step in range(STEPS):
        for out, in0, in1 in ((a, y, y), (a, a, hv), (a, a, None), (y, y, a)):
            if in1 is None:
                pool.sem_inc(passed, 1)
                ins = pool.tensor_scalar(out, in0, 1.5, None, ALU.add)
            else:
                ins = pool.tensor_tensor(out, in0, in1, ALU.mult)
            if step == STEPS - 1 and out is y:
                ins.then_inc(made, 1)
                return
            count[0] += 1
            ins.then_inc(chain, 1)
            pool.wait_ge(chain, count[0] if isinstance(count[1], int) else count[1] + count[0])


def gated_block(nc, x, ctx_t, g_xattn, g_ffn, wq_t, wk_t, wv_t, wo_t, bo, router, w_gate, w_up, w_down, out):
    with ExitStack() as both:
        ident = both.enter_context(nc.sbuf_tensor("ident", [P, P], F32))
        gates = both.enter_context(nc.sbuf_tensor("gates", [P, 2], F32))
        tanh_gates = both.enter_context(nc.sbuf_tensor("tanh_gates", [P, 2], F32))
        x1 = nc.dram_tensor("x1_between", [B * S, D], F32, kind="Internal").ap()
        with ExitStack() as ctx:
            attention(nc, ctx, x, ctx_t, g_xattn, g_ffn, wq_t, wk_t, wv_t, wo_t, bo, x1, ident, gates, tanh_gates)
        with ExitStack() as ctx:
            experts(nc, ctx, x1, router, w_gate, w_up, w_down, out, ident, tanh_gates)


def attention(nc, ctx, x, ctx_t, g_xattn, g_ffn, wq_t, wk_t, wv_t, wo_t, bo, x1, ident, gates, tanh_gates):
    def sb(name, shape, dt=F32):
        return ctx.enter_context(nc.sbuf_tensor(name, shape, dt))

    def sem(name):
        return ctx.enter_context(nc.semaphore(name))

    w_hi, w_lo = (sb(f"w_{n}", [P, 4, C, D], F32R) for n in ("hi", "lo"))
    WQ, WK, WV, WO = range(4)
    q_stack = [sb(f"q_stack{i}", [P, H, S], F32R) for i in range(2)]
    k_stack = [sb(f"k_stack{i}", [P, H, S], F32R) for i in range(2)]
    x_in = sb("x_in", [P, T, D])
    c_in = sb("c_in", [P, C, S])
    c_hi, c_lo = sb("c_hi", [P, C, S], F32R), sb("c_lo", [P, C, S], F32R)
    t_hi, t_lo = sb("t_hi", [P, C, S], F32R), sb("t_lo", [P, C, S], F32R)
    q_hi, q_lo = sb("q_hi", [P, C, S], F32R), sb("q_lo", [P, C, S], F32R)
    k_hi, k_lo = sb("k_hi", [P, C, S], F32R), sb("k_lo", [P, C, S], F32R)
    v_parts = [sb(f"v_parts{i}", [P, T, 3, D], BF16) for i in range(2)]
    v_rest = sb("v_rest", [P, D])
    RING = 4
    probs = [sb(f"probs{i}", [P, 3 * P]) for i in range(RING)]
    pt_hi = [sb(f"pt_hi{i}", [P, 3 * P], F16) for i in range(2)]
    pt_lo = [sb(f"pt_lo{i}", [P, 3 * P], F16) for i in range(2)]
    Y_LATE = 2
    y = sb("y", [P, Y_LATE + 1, T, D // 2])
    y_sum = sb("y_sum", [P, T * JH, DH])
    x_res = sb("x_res", [P, T, D])
    mask = sb("mask", [P, 2 * P])
    bias = sb("bias", [P, D])
    neg_max = sb("neg_max", [P, H, T])
    row_sum = sb("row_sum", [P, H, T])
    row_inv = sb("row_inv", [P, JH, T])
    stats, mv = sb("stats", [P, T, 6]), sb("mv", [P, T, 2])
    var_eps, shifted = sb("var_eps", [P, T]), sb("shifted", [P, T], I32)
    half_var, rstd, newton = sb("half_var", [P, T]), sb("rstd", [P, T]), sb("newton", [P, T])

    bank = [ctx.enter_context(nc.psum_tensor(f"bank{i}", [P, D], F32)) for i in range(2)]
    sc_ps = [ctx.enter_context(nc.psum_tensor(f"scores{i}", [P, T, S], F32)) for i in range(2)]
    pt_ps = [ctx.enter_context(nc.psum_tensor(f"probs_t{i}", [P, D], F32)) for i in range(2)]
    y_ps = [ctx.enter_context(nc.psum_tensor(f"y{i}", [P, T, JH, 2, DH], F32)) for i in range(2)]

    raw_loaded = [sem(f"raw_loaded{i}") for i in range(2)]
    small_loaded = sem("small_loaded")
    x_loaded, c_loaded, res_loaded = sem("x_loaded"), sem("c_loaded"), sem("res_loaded")
    stacked = [[sem(f"stacked{i}_{j}") for j in range(JH)] for i in range(2)]
    x1_stored = sem("x1_stored")
    ident_made, mask_made, bias_made = sem("ident_made"), sem("mask_made"), sem("bias_made")
    pool_chain, rstd_made, c_lo_made, v3_made = sem("pool_chain"), sem("rstd_made"), sem("c_lo_made"), sem("v3_made")
    res_made = sem("res_made")
    pool_passed, dve_passed, sp_passed = sem("pool_passed"), sem("dve_passed"), sem("sp_passed")
    w_hi_made, tanh_made, c_hi_made = sem("w_hi_made"), sem("tanh_made"), sem("c_hi_made")
    xt_hi_made, q_hi_made, k_hi_made = sem("xt_hi_made"), sem("q_hi_made"), sem("k_hi_made")
    v1_made, v2_made, yt_hi_made = sem("v1_made"), sem("v2_made"), sem("yt_hi_made")
    probs_made, pt_hi_made = sem("probs_made"), sem("pt_hi_made")
    w_lo_made, guess_made, norm_chain = sem("w_lo_made"), sem("guess_made"), sem("norm_chain")
    xn_made, group_chain = sem("xn_made"), sem("group_chain")
    xt_lo_made, q_lo_made, k_lo_made = sem("xt_lo_made"), sem("q_lo_made"), sem("k_lo_made")
    v_rest_made, yt_lo_made, x1_made = sem("v_rest_made"), sem("yt_lo_made"), sem("x1_made")
    max_made, pt_lo_made, y_made = sem("max_made"), sem("pt_lo_made"), sem("y_made")
    xt_done, q_done, k_done, v_done = sem("xt_done"), sem("q_done"), sem("k_done"), sem("v_done")
    yt_done, o_done = sem("yt_done"), sem("o_done")
    scores_done, pt_done, pv_done = sem("scores_done"), sem("pt_done"), sem("pv_done")

    x_v = x.rearrange("(b t p) d -> b p t d", p=P, t=T)
    x1_v = x1.rearrange("(b t p) d -> b p t d", p=P, t=T)
    c_v = ctx_t.rearrange("(c p) (b t) -> b p c t", p=P, b=B)
    w_v = [w.rearrange("(c p) o -> p c o", p=P) for w in (wq_t, wk_t, wv_t, wo_t)]
    HC = C // 2
    raw = [x_res[:], y[:, 0:2].rearrange("p y t (c d) -> p (y t c) d", c=1).rearrange("p (c a) d -> p c (a d)", c=HC)]
    RAW_ORDER = (WK, WQ, WV, WO)
    N_RAW = len(RAW_ORDER) * 2
    STACK_DMAS = 2 * 3
    PAIR = 2

    FIRST, PAIRS = 3, 5

    def iterations(eng, run):
        for i in range(-1, FIRST):
            run(At(0, 2, i))
        with eng.Fori(0, PAIRS) as r:
            for u in range(2):
                run(At(r, 2, FIRST + u))
        for i in range(FIRST + 2 * PAIRS, B + 1):
            run(At(0, 2, i))

    def has(i, ahead):
        return not isinstance(i.r, int) or 0 <= i.k + ahead < B

    def lagging(i, s, lag):
        back = s < lag
        if not has(i, -back):
            return None
        return i + (-1 if back else 0), (s - lag) % H

    TR_LAG, PV_LAG = 2, 3
    GROUP_LAG = PV_LAG + JH - 1
    BANK_A, BANK_B = 0, 1
    K_SLOTS, K_EVAC = (0, 1, 2, 3), (2, 4)
    X_SLOTS, X_EVAC, X_BANKS = (0, 2), (1, 3), (BANK_B, BANK_A)
    Q_SLOTS, Q_EVAC = (4, 5, 6, 7), (6, 8)
    V_SLOTS, V_EVAC, V_SPLIT = ((8, 9), (10, 11)), (10, 12), (11, 13)
    Y_SLOTS, Y_EVAC, Y_BANKS = (8, 10), (9, 11), (BANK_B, BANK_A)
    O_SLOTS, O_EVAC = ((12, 13), (14, 15)), (14, 15)
    RES_SLOT, LN_SLOT, C_SLOT, XN_SLOT = 6, 7, 12, 13

    with nc.Block() as block:
        @block.sync
        def _(sp):
            sp.dma_start(x_in[:], x_v[0]).then_inc(x_loaded, DMA)
            sp.dma_start(c_in[:], c_v[0]).then_inc(c_loaded, DMA)
            for n in range(N_RAW):
                wait(sp, w_lo_made, n - 1)
                src = w_v[RAW_ORDER[n // 2]][:, (n % 2) * HC:(n % 2 + 1) * HC, :]
                sp.dma_start(raw[n % 2], src).then_inc(raw_loaded[n % 2], DMA)
                if n == 1:
                    sp.dma_start(gates[:, 0:1], g_xattn.partition_broadcast(P)).then_inc(small_loaded, DMA)
                    sp.dma_start(gates[:, 1:2], g_ffn.partition_broadcast(P)).then_inc(small_loaded, DMA)
                    sp.dma_start(bias[:], bo.partition_broadcast(P)).then_inc(small_loaded, DMA)
                if n == 3:
                    sp.wait_ge(c_lo_made, 1)
                    sp.dma_start(c_in[:], c_v[1]).then_inc(c_loaded, DMA)

            def stack(dst, j, group, src):
                lo, hi = group * DH, (group + 1) * DH
                return sp.dma_start(dst[lo:hi, j:H:JH, :].bitcast(F32), src[j * DH:(j + 1) * DH].bitcast(F32))

            def run(i):
                n, o, ln, far = i + 1, i + -1, i + 2, i + 3
                par = n.parity()
                if has(i, -1):
                    wait(sp, x1_stored, o.times(DMA))
                    sp.dma_start(x_res[:], row(x_v, o)).then_inc(res_loaded, DMA)
                if has(i, 2):
                    sp.wait_ge(xt_done, ln.times(T))
                    sp.dma_start(x_in[:], row(x_v, ln)).then_inc(x_loaded, DMA)
                if has(i, 1):
                    wait(sp, scores_done, n.times(H, -H))
                    sp.sem_inc(sp_passed, 1)
                    sp.wait_ge(k_lo_made, n.times(2, 2))
                    for j in range(JH):
                        stack(k_stack[par], j, 0, k_hi).then_inc(stacked[par][j], DMA)
                        stack(k_stack[par], j, 1, k_hi).then_inc(stacked[par][j], DMA)
                        stack(k_stack[par], j, 2, k_lo).then_inc(stacked[par][j], DMA)
                if has(i, 1):
                    sp.wait_ge(q_lo_made, n.times(2, 2))
                    for j in range(JH):
                        stack(q_stack[par], j, 0, q_hi).then_inc(stacked[par][j], DMA)
                        stack(q_stack[par], j, 1, q_lo).then_inc(stacked[par][j], DMA)
                        stack(q_stack[par], j, 2, q_hi).then_inc(stacked[par][j], DMA)
                if has(i, 3):
                    sp.wait_ge(c_lo_made, far.times(1))
                    sp.dma_start(c_in[:], row(c_v, far)).then_inc(c_loaded, DMA)
                if has(i, -1):
                    sp.wait_ge(x1_made, o.times(T, T))
                    sp.dma_start(row(x1_v, o), x_res[:]).then_inc(x1_stored, DMA)

            sp.wait_ge(w_lo_made, N_RAW)
            iterations(sp, run)
            sp.wait_ge(x1_stored, B * DMA)

        @block.gpsimd
        def _(pool):
            pool.memset(ident[:], 0.0).then_inc(pool_chain, 1)
            pool.memset(mask[:], 0.0).then_inc(pool_chain, 1)
            pool.wait_ge(pool_chain, 2)
            pool.affine_select(out=ident[:], in_=ident[:], compare_op=ALU.not_equal, fill=1.0, base=0,
                               pattern=[[-1, P]], channel_multiplier=1).then_inc(ident_made, 1)
            pool.affine_select(out=mask[:, P:], in_=mask[:, P:], compare_op=ALU.is_ge, fill=NEG, base=0,
                               pattern=[[-1, P]], channel_multiplier=1).then_inc(mask_made, 1)
            NEWTON = 11

            def inverse_std(ln):
                pool.wait_ge(guess_made, ln.times(1, 1))
                first = 2 + NEWTON * ln.k
                base = 0 if isinstance(ln.r, int) else ln.r * (NEWTON * ln.step)
                newton_rsqrt(pool, pool_chain, pool_passed, [first, base], rstd[:], half_var[:], newton[:], rstd_made)

            def context_lo(n):
                pool.wait_ge(c_hi_made, n.times(1, 1))
                pool.tensor_tensor(c_lo[:], c_in[:], c_hi[:].bitcast(F32), ALU.subtract).then_inc(c_lo_made, 1)

            def run(i):
                n, o, ln = i + 1, i + -1, i + 2
                for s in range(H):
                    if s in V_SPLIT and has(i, 1):
                        t, parts = V_SPLIT.index(s), v_parts[n.parity()]
                        pool.wait_ge(v2_made, n.times(T, t + 1))
                        pool.tensor_tensor(parts[:, t, 2, :], v_rest[:], parts[:, t, 1, :], ALU.subtract).then_inc(v3_made, 1)
                    if s == C_SLOT and has(i, 2):
                        context_lo(ln)
                    if s == RES_SLOT and has(i, -1):
                        pool.wait_ge(res_loaded, o.times(DMA, DMA))
                        for t in range(T):
                            pool.tensor_tensor(x_res[:, t, :], x_res[:, t, :], bias[:], ALU.add).then_inc(res_made, 1)
                    if s == LN_SLOT and has(i, 2):
                        inverse_std(ln)

            context_lo(At(0, 2, 0))
            inverse_std(At(0, 2, 0))
            pool.wait_ge(small_loaded, 3 * DMA)
            pool.wait_ge(tanh_made, 1)
            pool.tensor_scalar(bias[:], bias[:], tanh_gates[:, 0:1], None, ALU.mult).then_inc(bias_made, 1)
            pool.wait_ge(bias_made, 1)
            iterations(pool, run)

        @block.scalar
        def _(act):
            def context_hi(n):
                act.wait_ge(c_loaded, n.times(DMA, DMA))
                wait(act, v_done, n.times(T))
                act.copy(c_hi[:], c_in[:]).then_inc(c_hi_made, 1)

            context_hi(At(0, 2, 0))
            for n in range(N_RAW):
                act.wait_ge(raw_loaded[n % 2], (n // 2 + 1) * DMA)
                act.copy(w_hi[:, RAW_ORDER[n // 2], (n % 2) * HC:(n % 2 + 1) * HC, :], raw[n % 2]).then_inc(w_hi_made, 1)
                if n == 3:
                    act.wait_ge(small_loaded, 3 * DMA)
                    act.activation(tanh_gates[:], gates[:], ACT.Tanh).then_inc(tanh_made, 1)

            def rows_hi(t, b, made):
                act.copy(t_hi[:, :, t * P:(t + 1) * P], bank[b][:].rearrange("p (c t) -> p c t", c=C)).then_inc(made, 1)

            def run(i):
                n, o, ln = i + 1, i + -1, i + 2
                for s in range(H):
                    if has(i, 1):
                        if s in V_EVAC:
                            t, parts = V_EVAC.index(s), v_parts[n.parity()]
                            act.wait_ge(v_done, n.times(T, t + 1))
                            if t == 0:
                                wait(act, pv_done, n.times(H, -H))
                            act.copy(parts[:, t, 0, :], bank[t][:]).then_inc(v1_made, 1)
                        if s in V_SPLIT:
                            t, parts = V_SPLIT.index(s), v_parts[n.parity()]
                            act.wait_ge(v_rest_made, n.times(T, t + 1))
                            act.copy(parts[:, t, 1, :], v_rest[:]).then_inc(v2_made, 1)
                        if s in X_EVAC:
                            t = X_EVAC.index(s)
                            act.wait_ge(xt_done, n.times(T, t + 1))
                            if t == 0:
                                wait(act, q_done, n.times(2))
                                wait(act, o_done, n.times(T, -2 * T))
                            rows_hi(t, X_BANKS[t], xt_hi_made)
                        for slots, hi, done, made in ((Q_EVAC, q_hi, q_done, q_hi_made), (K_EVAC, k_hi, k_done, k_hi_made)):
                            if s in slots:
                                u = slots.index(s)
                                act.wait_ge(done, n.times(2, u + 1))
                                if u == 0 and (not isinstance(n.r, int) or n.k > 0):
                                    m = n + -1
                                    for j in range(JH):
                                        act.wait_ge(stacked[m.parity()][j], m.over(2).times(STACK_DMAS * DMA, STACK_DMAS * DMA))
                                act.copy(hi[:, PAIR * u:PAIR * (u + 1), :],
                                         bank[u][:].rearrange("p (m t) -> p m t", m=PAIR)).then_inc(made, 1)
                    if s in Y_EVAC and has(i, -1):
                        t = Y_EVAC.index(s)
                        act.wait_ge(yt_done, o.times(T, t + 1))
                        if t == 0 and has(i, 1):
                            act.wait_ge(q_done, n.times(2, 2))
                        elif t == 0:
                            wait(act, o_done, o.times(T))
                        rows_hi(t, Y_BANKS[t], yt_hi_made)
                    if (bh := lagging(i, s, TR_LAG)):
                        b, h = bh
                        act.wait_ge(pt_done, b.times(H, h + 1))
                        wait(act, pv_done, b.times(H, h - 1))
                        act.copy(pt_hi[h % 2][:], pt_ps[h % 2][:, 0:3 * P]).then_inc(pt_hi_made, 1)
                    if has(i, 0):
                        act.wait_ge(max_made, i.times(H, s + 1))
                        p = probs[s % RING]
                        act.activation(p[:, 0:P], p[:, 0:P], ACT.Exp, bias=neg_max[:, s, 0:1],
                                       scale=-1.0, accum_out=row_sum[:, s, 0:1])
                        act.activation(p[:, P:], p[:, P:], ACT.Exp, bias=neg_max[:, s, 1:2],
                                       scale=-1.0, accum_out=row_sum[:, s, 1:2]).then_inc(probs_made, 1)
                    if s == C_SLOT and has(i, 2):
                        context_hi(ln)

            iterations(act, run)

        @block.vector
        def _(dve):
            NORM_STEPS = 2 * T + 2
            PER_GROUP = 2

            def statistics(ln):
                dve.wait_ge(x_loaded, ln.times(DMA, DMA))
                for t in range(T):
                    dve.bn_stats(stats[:, t, :], x_in[:, t, :]).then_inc(norm_chain, 1)
                dve.wait_ge(norm_chain, ln.times(NORM_STEPS, T))
                wait(dve, xn_made, ln.times(T))
                dve.sem_inc(dve_passed, 1)
                for t in range(T):
                    dve.bn_aggr(mv[:, t, :], stats[:, t, :]).then_inc(norm_chain, 1)
                dve.wait_ge(norm_chain, ln.times(NORM_STEPS, 2 * T))
                dve.tensor_scalar(var_eps[:], mv[:, :, 1], EPS, None, ALU.add).then_inc(norm_chain, 1)
                dve.wait_ge(norm_chain, ln.times(NORM_STEPS, 2 * T + 1))
                dve.tensor_scalar(shifted[:], var_eps[:].bitcast(I32), 1, None,
                                  ALU.logical_shift_right).then_inc(norm_chain, 1)
                dve.tensor_scalar(half_var[:], var_eps[:], -0.5, None, ALU.mult)
                dve.wait_ge(norm_chain, ln.times(NORM_STEPS, 2 * T + 2))
                dve.tensor_scalar(rstd[:].bitcast(I32), shifted[:], -1.0, RSQRT_MAGIC, ALU.mult,
                                  ALU.add).then_inc(guess_made, 1)

            def normalise(ln):
                dve.wait_ge(rstd_made, ln.times(1, 1))
                for t in range(T):
                    dve.tensor_scalar(x_in[:, t, :], x_in[:, t, :], mv[:, t, 0:1], rstd[:, t:t + 1],
                                      ALU.subtract, ALU.mult).then_inc(xn_made, 1)

            statistics(At(0, 2, 0))
            for n in range(N_RAW):
                dve.wait_ge(w_hi_made, n + 1)
                part = w_lo[:, RAW_ORDER[n // 2], (n % 2) * HC:(n % 2 + 1) * HC, :]
                upper = w_hi[:, RAW_ORDER[n // 2], (n % 2) * HC:(n % 2 + 1) * HC, :].bitcast(F32)
                dve.tensor_tensor(part, raw[n % 2], upper, ALU.subtract).then_inc(w_lo_made, 1)
                if n == 1:
                    normalise(At(0, 2, 0))
            dve.wait_ge(mask_made, 1)

            def rows_lo(t, b, made):
                part = slice(t * P, (t + 1) * P)
                dve.tensor_tensor(t_lo[:, :, part], bank[b][:].rearrange("p (c t) -> p c t", c=C),
                                  t_hi[:, :, part].bitcast(F32), ALU.subtract).then_inc(made, 1)

            def close_group(b, g):
                steps = PER_GROUP * (H // JH)
                first, heads = PER_GROUP * g, slice(JH * g, JH * (g + 1))
                dve.wait_ge(pv_done, b.times(H, JH * (g + 1)))
                if g in (0, 2):
                    wait(dve, yt_done, b.times(T, -T if g == 0 else 0))
                    if g == 0 and isinstance(b.r, int) and b.k == 0:
                        dve.wait_ge(w_lo_made, N_RAW)
                dve.reciprocal(row_inv[:], row_sum[:, heads, :]).then_inc(group_chain, 1)
                dve.tensor_reduce(y_sum[:], y_ps[g % 2][:].rearrange("p t h x d -> p (t h) d x"), AX.X,
                                  ALU.add).then_inc(group_chain, 1)
                dve.wait_ge(group_chain, b.times(steps, first + PER_GROUP))
                part, at = (b.parity(), g * P) if g < 2 else (Y_LATE, (g - 2) * P)
                dve.tensor_tensor(y[:, part, :, at:at + P].rearrange("p t (h d) -> p t h d", d=DH),
                                  y_sum[:].rearrange("p (t h) d -> p t h d", t=T),
                                  row_inv[:].rearrange("p h t -> p t h").unsqueeze(3).to_broadcast([P, T, JH, DH]),
                                  ALU.mult).then_inc(y_made, 1)

            def residual(o, t):
                dve.wait_ge(o_done, o.times(T, t + 1))
                dve.wait_ge(res_made, o.times(T, t + 1))
                dve.scalar_tensor_tensor(out=x_res[:, t, :], in0=bank[t][:], scalar=tanh_gates[:, 0:1],
                                         in1=x_res[:, t, :], op0=ALU.mult, op1=ALU.add).then_inc(x1_made, 1)

            def run(i):
                n, o, ln = i + 1, i + -1, i + 2
                for s in range(H):
                    if has(i, 0):
                        dve.wait_ge(scores_done, i.times(H, s + 1))
                        wait(dve, pt_done, i.times(H, s - RING + 1))
                        dve.sem_inc(dve_passed, 1)
                        p = probs[s % RING]
                        for t in range(T):
                            keys = slice(0, P * (t + 1))
                            dst = p[:, 0:P] if t == 0 else p[:, P:]
                            ins = dve.tensor_tensor_reduce(dst, sc_ps[s % 2][:, t, keys], mask[:, P * (1 - t):], -SCALE, -NEG,
                                                           ALU.add, ALU.min, neg_max[:, s, t:t + 1])
                        ins.then_inc(max_made, 1)
                    if has(i, 1):
                        if s in V_EVAC:
                            t = V_EVAC.index(s)
                            dve.wait_ge(v1_made, n.times(T, t + 1))
                            wait(dve, v3_made, n.times(T, t))
                            dve.tensor_tensor(v_rest[:], bank[t][:], v_parts[n.parity()][:, t, 0, :],
                                              ALU.subtract).then_inc(v_rest_made, 1)
                        if s in X_EVAC:
                            t = X_EVAC.index(s)
                            dve.wait_ge(xt_hi_made, n.times(T, t + 1))
                            rows_lo(t, X_BANKS[t], xt_lo_made)
                        for slots, hi, lo, hi_made, made in ((Q_EVAC, q_hi, q_lo, q_hi_made, q_lo_made),
                                                             (K_EVAC, k_hi, k_lo, k_hi_made, k_lo_made)):
                            if s in slots:
                                u = slots.index(s)
                                part = slice(PAIR * u, PAIR * (u + 1))
                                dve.wait_ge(hi_made, n.times(2, u + 1))
                                dve.tensor_tensor(lo[:, part, :], bank[u][:].rearrange("p (m t) -> p m t", m=PAIR),
                                                  hi[:, part, :].bitcast(F32), ALU.subtract).then_inc(made, 1)
                    if has(i, -1):
                        if s in Y_EVAC:
                            t = Y_EVAC.index(s)
                            dve.wait_ge(yt_hi_made, o.times(T, t + 1))
                            rows_lo(t, Y_BANKS[t], yt_lo_made)
                        if s == O_EVAC[0]:
                            residual(o, 0)
                    if (bh := lagging(i, s, TR_LAG)):
                        b, h = bh
                        dve.wait_ge(pt_hi_made, b.times(H, h + 1))
                        dve.tensor_tensor(pt_lo[h % 2][:], pt_ps[h % 2][:, 0:3 * P], pt_hi[h % 2][:],
                                          ALU.subtract).then_inc(pt_lo_made, 1)
                    if (bh := lagging(i, s, GROUP_LAG)) and bh[1] % JH == 0:
                        close_group(bh[0], bh[1] // JH)
                    if s == LN_SLOT and has(i, 2):
                        statistics(ln)
                    if s == XN_SLOT and has(i, 2):
                        normalise(ln)
                    if s == O_EVAC[1] and has(i, -1):
                        residual(o, 1)

            iterations(dve, run)

        @block.tensor
        def _(pe):
            pe.wait_ge(ident_made, 1)
            PASSES = ((0, 0), (1, 0), (0, 1))
            HALF_CHUNKS = (range(0, C // 2), range(C // 2, C))

            def transpose_rows(chunk, dst):
                for c in range(C):
                    ins = pe.transpose(dst[:, c * P:(c + 1) * P], chunk(c), ident[:])
                return ins

            def y_chunk(b, t, c):
                return y[:, b.parity() if c < 2 else Y_LATE, t, c % 2 * P:(c % 2 + 1) * P]

            def three_pass(dst, stationary, moving, chunks=range(C)):
                for c in chunks:
                    for k, (a, b) in enumerate(PASSES):
                        ins = pe.matmul(dst, stationary[a](c), moving[b](c), start=(c == 0 and k == 0),
                                        stop=(c == C - 1 and k == len(PASSES) - 1))
                return ins

            def weight(mat, lo=0, hi=D):
                return lambda c: w_hi[:, mat, c, lo:hi], lambda c: w_lo[:, mat, c, lo:hi]

            def rows(hi, lo, part=slice(0, S)):
                return lambda c: hi[:, c, part], lambda c: lo[:, c, part]

            def tile(t):
                return slice(t * P, (t + 1) * P)

            def split(mat, first):
                wait(pe, w_lo_made, 2 * RAW_ORDER.index(mat) + 2 if first else 0)

            def project(m, mat, src, done):
                ins = three_pass(bank[m // PAIR][:, (m % PAIR) * S:(m % PAIR + 1) * S],
                                 weight(mat, m * P, (m + 1) * P), src)
                if m % PAIR == PAIR - 1:
                    ins.then_inc(done, 1)

            def units(i, s):
                n, o = i + 1, i + -1
                first = isinstance(n.r, int) and n.k == 0
                if has(i, 1):
                    if s in K_SLOTS:
                        m = K_SLOTS.index(s)
                        if m == 0:
                            pe.wait_ge(c_lo_made, n.times(1, 1))
                            split(WK, first)
                            wait(pe, x1_made, n.times(T, 1 - 3 * T))
                        elif m == PAIR:
                            pe.wait_ge(xt_lo_made, n.times(T, 1))
                        project(m, WK, rows(c_hi, c_lo), k_done)
                    if s in X_SLOTS:
                        t = X_SLOTS.index(s)
                        pe.wait_ge(xn_made, n.times(T, t + 1))
                        if t == 0:
                            wait(pe, x1_made, n.times(T, 2 - 3 * T))
                        else:
                            pe.wait_ge(k_lo_made, n.times(2, 1))
                        transpose_rows(lambda c: x_in[:, t, c * P:(c + 1) * P], bank[X_BANKS[t]]).then_inc(xt_done, 1)
                    if s in Q_SLOTS:
                        m = Q_SLOTS.index(s)
                        if m == 0:
                            split(WQ, first)
                            pe.wait_ge(xt_lo_made, n.times(T, T))
                        elif m == PAIR:
                            pe.wait_ge(k_lo_made, n.times(2, 2))
                        project(m, WQ, rows(t_hi, t_lo), q_done)
                    for t in range(T):
                        if s in V_SLOTS[t]:
                            half = V_SLOTS[t].index(s)
                            if half == 0 and t == 0:
                                split(WV, first)
                                pe.wait_ge(q_lo_made, n.times(2, 1))
                            elif half == 0 and has(i, -1):
                                pe.wait_ge(yt_lo_made, o.times(T, 1))
                            elif half == 0:
                                pe.wait_ge(q_lo_made, n.times(2, 2))
                            ins = three_pass(bank[t][:], rows(c_hi, c_lo, tile(t)), weight(WV), HALF_CHUNKS[half])
                            if half == 1:
                                ins.then_inc(v_done, 1)
                if has(i, -1):
                    if s in Y_SLOTS:
                        t = Y_SLOTS.index(s)
                        if t == 0:
                            pe.wait_ge(y_made, o.times(H // JH, H // JH))
                        if has(i, 1) and t == 0:
                            pe.wait_ge(q_lo_made, n.times(2, 2))
                        elif has(i, 1):
                            pe.wait_ge(v_rest_made, n.times(T, 1))
                        else:
                            wait(pe, x1_made, o.times(T, (0, 1 - T)[t]))
                        transpose_rows(lambda c: y_chunk(o, t, c), bank[Y_BANKS[t]]).then_inc(yt_done, 1)
                    for t in range(T):
                        if s in O_SLOTS[t]:
                            half = O_SLOTS[t].index(s)
                            if half == 0 and t == 0:
                                split(WO, isinstance(o.r, int) and o.k == 0)
                                pe.wait_ge(yt_lo_made, o.times(T, T))
                            elif half == 0 and has(i, 1):
                                pe.wait_ge(v_rest_made, n.times(T, T))
                            ins = three_pass(bank[t][:], rows(t_hi, t_lo, tile(t)), weight(WO), HALF_CHUNKS[half])
                            if half == 1:
                                ins.then_inc(o_done, 1)

            def run(i):
                for s in range(H):
                    if has(i, 0):
                        par = i.parity()
                        if s < JH:
                            pe.wait_ge(stacked[par][s], i.over(2).times(STACK_DMAS * DMA, STACK_DMAS * DMA))
                        wait(pe, max_made, i.times(H, s - 1))
                        pairs = slice(0, 3 * DH)
                        for t in range(T):
                            ins = pe.matmul(sc_ps[s % 2][:, t, :], q_stack[par][pairs, s, tile(t)],
                                            k_stack[par][pairs, s, :], start=True, stop=True)
                        ins.then_inc(scores_done, 1)
                    if (bh := lagging(i, s, PV_LAG)):
                        b, h = bh
                        g, hg, v = h // JH, h % JH, v_parts[b.parity()]
                        if h == 0:
                            pe.wait_ge(v3_made, b.times(T, T))
                        if hg == 0:
                            wait(pe, y_made, b.times(H // JH, g - 1))
                        pe.wait_ge(pt_lo_made, b.times(H, h + 1))
                        col = slice(h * DH, (h + 1) * DH)
                        for t, blocks in ((0, ((0, 0),)), (1, ((1, 0), (2, 1)))):
                            for k, (blk, key) in enumerate(blocks):
                                last = k == len(blocks) - 1
                                dst = y_ps[g % 2][:, t, hg]
                                pe.matmul(dst, pt_hi[h % 2][:, tile(blk)], v[:, key, 0:2, col], start=(k == 0), stop=False)
                                pe.matmul(dst[:, 1], pt_hi[h % 2][:, tile(blk)], v[:, key, 2, col], start=False, stop=False)
                                ins = pe.matmul(dst, pt_lo[h % 2][:, tile(blk)], v[:, key, 0:2, col], start=False, stop=last)
                        ins.then_inc(pv_done, 1)
                    if (bh := lagging(i, s, TR_LAG)):
                        b, h = bh
                        pe.wait_ge(probs_made, b.times(H, h + 1))
                        wait(pe, pt_lo_made, b.times(H, h - 1))
                        for k in range(3):
                            ins = pe.transpose(pt_ps[h % 2][:, tile(k)], probs[h % RING][:, tile(k)], ident[:])
                        ins.then_inc(pt_done, 1)
                    units(i, s)

            iterations(pe, run)


def experts(nc, ctx, x1, router, w_gate, w_up, w_down, out, ident, tanh_gates):
    def sb(name, shape, dt=F32):
        return ctx.enter_context(nc.sbuf_tensor(name, shape, dt))

    def sem(name):
        return ctx.enter_context(nc.semaphore(name))

    HALVES, U = 2, 2
    STEPS = NE * NB
    TURN = U * NB
    WP = C * F
    GATE, UP, DOWN = range(3)

    xt_hi, xt_lo = sb("xt_hi", [P, NB, C, BLK], F32R), sb("xt_lo", [P, NB, C, BLK], F32R)
    SLOTS = NB + 1
    acc = sb("acc", [P, SLOTS, BT, D])
    w_raw = sb("w_raw", [P, 3, WP])
    e_hi = [sb(f"e_hi{i}", [P, 3, WP], F32R) for i in range(2)]
    e_lo = [sb(f"e_lo{i}", [P, 3, WP], F32R) for i in range(2)]
    h_hi = [sb(f"h_hi{i}", [P, FC, BLK], F32R) for i in range(2)]
    h_lo = [sb(f"h_lo{i}", [P, FC, BLK], F32R) for i in range(2)]
    silu = [sb(f"silu{i}", [P, BLK]) for i in range(FC)]
    h = [sb(f"h{i}", [P, BLK]) for i in range(FC)]
    xn = [sb(f"xn{i}", [P, D]) for i in range(2)]
    r_raw = sb("r_raw", [P, C, P])
    r_hi, r_lo = sb("r_hi", [P, C, P], F32R), sb("r_lo", [P, C, P], F32R)
    logits_t = sb("logits_t", [P, BLK])
    before = sb("before", [P, E, E])
    stats, mv = sb("norm_stats", [P, BT, 6]), sb("norm_mv", [P, BT, 2])
    var_eps, shifted = sb("norm_var_eps", [P, BT]), sb("norm_shifted", [P, BT], I32)
    half_var, rstd, newton = sb("norm_half_var", [P, BT]), sb("norm_rstd", [P, BT]), sb("norm_newton", [P, BT])
    top, total, inverse = sb("top", [P, BT]), sb("total", [P, BT]), sb("inverse", [P, BT])
    shift, weights, share = sb("shift", [P, BT, E]), sb("weights", [P, BT, E]), sb("share", [P, BT, E])
    rank = sb("rank", [P, BT, E])
    ahead, equal = sb("ahead", [P, BT, E, E]), sb("equal", [P, BT, E, E])
    scale = sb("scale", [P, HALVES * NB, BT, NE])

    gu_ps = [ctx.enter_context(nc.psum_tensor(f"gate_up{i}", [P, 2, BLK], F32)) for i in range(FC)]
    dn_ps = [ctx.enter_context(nc.psum_tensor(f"down{i}", [P, D], F32)) for i in range(BT)]

    raw_loaded = [sem(f"e_raw_loaded{i}") for i in range(3)]
    r_loaded = sem("r_loaded")
    x1_loaded = [sem(f"x1_loaded{i}") for i in range(HALVES * NB)]
    stored = sem("stored")
    e_rstd_made = sem("e_rstd_made")
    e_pool_passed = sem("e_pool_passed")
    r_zeroed, before_made, e_pool_chain, e_xn_made = sem("r_zeroed"), sem("before_made"), sem("e_pool_chain"), sem("e_xn_made")
    silu_made, h_hi_made, e_hi_made = sem("silu_made"), sem("h_hi_made"), sem("e_hi_made")
    r_hi_made, e_xt_hi_made, logits_made, exp_made = sem("r_hi_made"), sem("e_xt_hi_made"), sem("logits_made"), sem("exp_made")
    h_made, h_lo_made, e_lo_made, added = sem("h_made"), sem("h_lo_made"), sem("e_lo_made"), sem("added")
    r_lo_made, e_guess_made, e_xt_lo_made = sem("r_lo_made"), sem("e_guess_made"), sem("e_xt_lo_made")
    shift_made, scale_made = sem("shift_made"), sem("scale_made")
    e_norm_chain, route_chain, shared_set = sem("e_norm_chain"), sem("route_chain"), sem("shared_set")
    gate_done, up_done, down_done = sem("gate_done"), sem("up_done"), sem("down_done")
    e_xt_done, logits_done, logits_back = sem("e_xt_done"), sem("logits_done"), sem("logits_back")

    x1_v = x1.rearrange("(k t p) d -> k p t d", p=P, t=BT)
    out_v = out.rearrange("(k t p) d -> k p t d", p=P, t=BT)
    g_v = w_gate.rearrange("e (c p) f -> e p c f", p=P)
    u_v = w_up.rearrange("e (c p) f -> e p c f", p=P)
    d_v = w_down.rearrange("e (f p) d -> e p f d", p=P)

    def piece(tile, which):
        part = tile[:, which, :]
        return part.rearrange("p (c f) -> p c f", c=FC if which == DOWN else C)

    def slot(k):
        return k % SLOTS

    def steps(eng, run, ready_last=lambda k: None):
        for half in range(HALVES):
            first, last = half * STEPS, (half + 1) * STEPS - TURN
            if half == 0:
                for n in range(TURN):
                    run(At(0, TURN, n), half)
                first += TURN
            with eng.Fori(0, (last - first) // TURN) as r:
                for k in range(TURN):
                    run(At(r, TURN, first + k), half)
            for n in range(last, last + TURN):
                run(At(0, TURN, n), half)
            if half + 1 < HALVES:
                ready_last((half + 2) * NB - 1)

    def follows(n):
        return not isinstance(n.r, int) or n.k < HALVES * STEPS - 1

    def readied(n, half):
        k = n.k - (half + 1) * STEPS
        return half * NB + NB + k + NB - 1 if isinstance(n.r, int) and half + 1 < HALVES and 1 - NB <= k < 0 else None

    with nc.Block() as block:
        @block.sync
        def _(sp):
            sp.wait_ge(r_zeroed, 1)
            sp.dma_start(r_raw[:, :, 0:E], router.rearrange("(c p) e -> p c e", p=P)).then_inc(r_loaded, DMA)

            def load_x1(k):
                sp.dma_start(acc[:, slot(k)], x1_v[k]).then_inc(x1_loaded[k], DMA)

            def load_raw(which, index):
                src = (g_v, u_v, d_v)[which]
                e = index if isinstance(index, int) else bass.ds(index, 1)
                src = src[e] if isinstance(index, int) else src[e].rearrange("o p c f -> (o p) c f")
                sp.dma_start(piece(w_raw, which), src).then_inc(raw_loaded[which], DMA)

            load_x1(0)
            for which in range(3):
                load_raw(which, 0)
            for k in range(1, NB):
                load_x1(k)
            for which in range(3):
                sp.wait_ge(e_lo_made, which + 1)
                load_raw(which, 1)
            load_x1(NB)

            def run(n, half):
                fixed, e, blk = isinstance(n.r, int), n.over(NB), n.k % NB
                if blk < 3 and (not fixed or e.k + 2 < HALVES * NE):
                    sp.wait_ge(e_lo_made, e.times(3, 3 + blk + 1))
                    within = At(e.r, e.step, e.k + 2 - half * NE).times(1)
                    load_raw(blk, within % NE if isinstance(within, int) else within)
                if fixed and n.k % STEPS >= STEPS - NB:
                    k = half * NB + blk
                    sp.wait_ge(added, BT * (n.k + 1))
                    sp.dma_start(out_v[k], acc[:, slot(k)]).then_inc(stored, DMA)
                    if half + 1 < HALVES and blk + 1 < NB:
                        sp.wait_ge(stored, DMA * (blk + 1))
                        load_x1(NB + blk + 1)

            steps(sp, run)
            sp.wait_ge(stored, HALVES * NB * DMA)

        @block.gpsimd
        def _(pool):
            pool.memset(r_raw[:], 0.0).then_inc(r_zeroed, 1)
            pool.memset(before[:], 1.0).then_inc(e_pool_chain, 1)
            pool.wait_ge(e_pool_chain, 1)
            pool.affine_select(out=before[:], in_=before[:], compare_op=ALU.is_gt, fill=0.0, base=0,
                               pattern=[[1, E], [-1, E]], channel_multiplier=0).then_inc(before_made, 1)

            def normalise(k):
                pool.wait_ge(e_guess_made, k + 1)
                newton_rsqrt(pool, e_pool_chain, e_pool_passed, [1 + 11 * k, 0], rstd[:], half_var[:], newton[:], e_rstd_made)
                pool.wait_ge(e_rstd_made, k + 1)
                for t in range(BT):
                    wait(pool, e_xt_done, BT * k + t - 1)
                    pool.tensor_scalar(xn[t % 2][:], acc[:, slot(k), t, :], mv[:, t, 0:1], rstd[:, t:t + 1],
                                       ALU.subtract, ALU.mult).then_inc(e_xn_made, 1)

            for k in range(HALVES * NB):
                normalise(k)

        @block.scalar
        def _(act):
            def split_hi(e, which):
                act.wait_ge(raw_loaded[which], e.times(DMA, DMA))
                if which != DOWN:
                    wait(act, up_done, e.times(NB * FC, -NB * FC))
                else:
                    wait(act, down_done, e.times(NB * BT, -NB * BT))
                act.copy(e_hi[e.parity()][:, which, :], w_raw[:, which, :]).then_inc(e_hi_made, 1)

            def rows_hi(k):
                for t in range(BT):
                    act.wait_ge(e_xt_done, BT * k + t + 1)
                    if k >= NB and t == 0:
                        act.wait_ge(up_done, FC * (STEPS - NB + k % NB + 1))
                    act.copy(xt_hi[:, k % NB, :, t * P:(t + 1) * P],
                             dn_ps[t][:].rearrange("p (c t) -> p c t", c=C)).then_inc(e_xt_hi_made, 1)

            def copy_logits(k, ps):
                act.wait_ge(logits_done, k + 1)
                act.copy(logits_t[:], ps).then_inc(logits_made, 1)

            def exponentials(k):
                act.wait_ge(shift_made, k + 1)
                act.activation(weights[:], shift[:], ACT.Exp).then_inc(exp_made, 1)

            def hidden(n):
                for f in range(FC):
                    act.wait_ge(gate_done, n.times(FC, f + 1))
                    wait(act, h_made, n.times(FC, f + 1 - FC))
                    act.activation(silu[f][:], gu_ps[f][:, 0, :], ACT.Silu).then_inc(silu_made, 1)
                    act.wait_ge(h_made, n.times(FC, f + 1))
                    wait(act, down_done, n.times(BT, -BT))
                    act.copy(h_hi[n.parity()][:, f, :], h[f][:]).then_inc(h_hi_made, 1)

            def ready(k):
                rows_hi(k)
                copy_logits(k, dn_ps[0][:])
                exponentials(k)

            def run(n, half):
                k = readied(n, half)
                if k is not None:
                    ready(k)
                if follows(n):
                    hidden(n + 1)
                e, blk = n.over(NB) + 1, n.k % NB
                if blk < 3 and (not isinstance(n.r, int) or e.k < HALVES * NE):
                    split_hi(e, blk)

            act.wait_ge(r_loaded, DMA)
            act.copy(r_hi[:], r_raw[:]).then_inc(r_hi_made, 1)
            for which in range(3):
                split_hi(At(0, U, 0), which)
            for k in range(NB):
                rows_hi(k)
                copy_logits(k, gu_ps[0][:, 0, :])
                exponentials(k)
            hidden(At(0, TURN, 0))
            steps(act, run, ready)

        @block.vector
        def _(dve):
            NORM_STEPS, ROUTE_STEPS = 2 * BT + 2, 10

            def split_lo(e, which):
                dve.wait_ge(e_hi_made, e.times(3, which + 1))
                dve.tensor_tensor(e_lo[e.parity()][:, which, :], w_raw[:, which, :],
                                  e_hi[e.parity()][:, which, :].bitcast(F32), ALU.subtract).then_inc(e_lo_made, 1)

            def statistics(k):
                at = NORM_STEPS * k
                dve.wait_ge(x1_loaded[k], DMA)
                for t in range(BT):
                    dve.bn_stats(stats[:, t, :], acc[:, slot(k), t, :]).then_inc(e_norm_chain, 1)
                dve.wait_ge(e_norm_chain, at + BT)
                wait(dve, e_xn_made, BT * k)
                for t in range(BT):
                    dve.bn_aggr(mv[:, t, :], stats[:, t, :]).then_inc(e_norm_chain, 1)
                dve.wait_ge(e_norm_chain, at + 2 * BT)
                dve.tensor_scalar(var_eps[:], mv[:, :, 1], EPS, None, ALU.add).then_inc(e_norm_chain, 1)
                dve.wait_ge(e_norm_chain, at + 2 * BT + 1)
                dve.tensor_scalar(shifted[:], var_eps[:].bitcast(I32), 1, None,
                                  ALU.logical_shift_right).then_inc(e_norm_chain, 1)
                dve.tensor_scalar(half_var[:], var_eps[:], -0.5, None, ALU.mult)
                dve.wait_ge(e_norm_chain, at + 2 * BT + 2)
                dve.tensor_scalar(rstd[:].bitcast(I32), shifted[:], -1.0, RSQRT_MAGIC, ALU.mult,
                                  ALU.add).then_inc(e_guess_made, 1)

            def rows_lo(k):
                for t in range(BT):
                    part = slice(t * P, (t + 1) * P)
                    dve.wait_ge(e_xt_hi_made, BT * k + t + 1)
                    dve.tensor_tensor(xt_lo[:, k % NB, :, part], dn_ps[t][:].rearrange("p (c t) -> p c t", c=C),
                                      xt_hi[:, k % NB, :, part].bitcast(F32), ALU.subtract).then_inc(e_xt_lo_made, 1)

            def route(k, ps):
                count = [ROUTE_STEPS * k]

                def link(ins):
                    count[0] += 1
                    ins.then_inc(route_chain, 1)
                    dve.wait_ge(route_chain, count[0])

                logits = ps.rearrange("p (t e) -> p t e", t=BT)[:, :, 0:E]
                wide, pairs = [P, BT, E], [P, BT, E, E]
                dve.wait_ge(logits_back, k + 1)
                link(dve.tensor_reduce(top[:], logits, AX.X, ALU.max))
                dve.tensor_tensor(shift[:], logits, top[:].unsqueeze(2).to_broadcast(wide),
                                  ALU.subtract).then_inc(shift_made, 1)
                dve.wait_ge(exp_made, k + 1)
                link(dve.tensor_reduce(total[:], weights[:], AX.X, ALU.add))
                link(dve.reciprocal(inverse[:], total[:]))
                link(dve.tensor_tensor(share[:], weights[:], inverse[:].unsqueeze(2).to_broadcast(wide), ALU.mult))
                mine, others = share[:].unsqueeze(3).to_broadcast(pairs), share[:].unsqueeze(2).to_broadcast(pairs)
                link(dve.tensor_tensor(ahead[:], others, mine, ALU.is_gt))
                link(dve.tensor_tensor(equal[:], others, mine, ALU.is_equal))
                link(dve.tensor_tensor(equal[:], equal[:], before[:].unsqueeze(1).to_broadcast(pairs), ALU.mult))
                link(dve.tensor_tensor(ahead[:], ahead[:], equal[:], ALU.add))
                link(dve.tensor_reduce(rank[:], ahead[:], AX.X, ALU.add))
                link(dve.scalar_tensor_tensor(out=rank[:], in0=rank[:], scalar=TOP - 0.5, in1=share[:],
                                              op0=ALU.is_lt, op1=ALU.mult))
                dve.tensor_scalar(scale[:, k, :, 0:E], rank[:], tanh_gates[:, 1:2], None, ALU.mult).then_inc(scale_made, 1)

            def hidden(n):
                for f in range(FC):
                    dve.wait_ge(up_done, n.times(FC, f + 1))
                    dve.wait_ge(silu_made, n.times(FC, f + 1))
                    wait(dve, h_lo_made, n.times(FC, f + 1 - FC))
                    dve.tensor_tensor(h[f][:], gu_ps[f][:, 1, :], silu[f][:], ALU.mult).then_inc(h_made, 1)
                    dve.wait_ge(h_hi_made, n.times(FC, f + 1))
                    dve.tensor_tensor(h_lo[n.parity()][:, f, :], h[f][:], h_hi[n.parity()][:, f, :].bitcast(F32),
                                      ALU.subtract).then_inc(h_lo_made, 1)

            def add(n, half):
                blk = n.k % NB
                e = At(n.r, U, (n.k - half * STEPS) // NB).times(1)
                k = half * NB + blk
                wait(dve, added, n.times(BT))
                for t in range(BT):
                    dve.wait_ge(down_done, n.times(BT, t + 1))
                    share_of = scale[:, k, t, e:e + 1] if isinstance(e, int) else scale[:, k, t, bass.ds(e, 1)]
                    dve.scalar_tensor_tensor(out=acc[:, slot(k), t, :], in0=dn_ps[t][:], scalar=share_of,
                                             in1=acc[:, slot(k), t, :], op0=ALU.mult, op1=ALU.add).then_inc(added, 1)

            def ready_last(k):
                statistics(k)
                rows_lo(k)
                route(k, dn_ps[1][:])

            def run(n, half):
                k = readied(n, half)
                if k is not None:
                    rows_lo(k)
                    route(k, dn_ps[1][:])
                if follows(n):
                    hidden(n + 1)
                add(n, half)
                e, blk = n.over(NB) + 1, n.k % NB
                if blk < 3 and (not isinstance(n.r, int) or e.k < HALVES * NE):
                    split_lo(e, blk)
                following = readied(n + 1, half) if isinstance(n.r, int) else None
                if following is not None:
                    statistics(following)

            for k in range(HALVES * NB):
                ins = dve.tensor_copy(scale[:, k, :, E:], tanh_gates[:, 1:2].unsqueeze(2).to_broadcast([P, BT, NE - E]))
            ins.then_inc(shared_set, 1)
            dve.wait_ge(shared_set, 1)
            dve.wait_ge(before_made, 1)
            statistics(0)
            dve.wait_ge(r_hi_made, 1)
            dve.tensor_tensor(r_lo[:], r_raw[:], r_hi[:].bitcast(F32), ALU.subtract).then_inc(r_lo_made, 1)
            for which in range(3):
                split_lo(At(0, U, 0), which)
            for k in range(NB):
                rows_lo(k)
                if k + 1 < NB:
                    statistics(k + 1)
                route(k, gu_ps[0][:, 1, :])
            hidden(At(0, TURN, 0))
            steps(dve, run, ready_last)

        @block.tensor
        def _(pe):
            def rows(k, ready):
                for t in range(BT):
                    pe.wait_ge(e_xn_made, BT * k + t + 1)
                    if ready:
                        pe.wait_ge(added, ready + t + 1)
                    elif k:
                        pe.wait_ge(e_xt_lo_made, BT * (k - 1) + t + 1)
                    for c in range(C):
                        ins = pe.transpose(dn_ps[t][:, c * P:(c + 1) * P], xn[t % 2][:, c * P:(c + 1) * P], ident[:])
                    ins.then_inc(e_xt_done, 1)

            PASSES = ((0, 0), (1, 0), (0, 1))

            def logits(k, ps, ps_back):
                pe.wait_ge(e_xt_hi_made, BT * (k + 1))
                pe.wait_ge(e_xt_lo_made, BT * (k + 1))
                pe.wait_ge(r_lo_made, 1)
                wait(pe, scale_made, k)
                i = 0
                for c in range(C):
                    for a, b in PASSES:
                        ins = pe.matmul(ps, (r_hi, r_lo)[a][:, c, :], (xt_hi, xt_lo)[b][:, k % NB, c, :],
                                        start=(i == 0), stop=(i == len(PASSES) * C - 1))
                        i += 1
                ins.then_inc(logits_done, 1)
                pe.wait_ge(logits_made, k + 1)
                for t in range(BT):
                    ins = pe.transpose(ps_back[:, t * P:(t + 1) * P], logits_t[:, t * P:(t + 1) * P], ident[:])
                ins.then_inc(logits_back, 1)

            def gate_up(n):
                e, blk = n.over(NB), n.k % NB
                par = e.parity()
                if blk == 0:
                    pe.wait_ge(e_lo_made, e.times(3, 2))
                for f in range(FC):
                    wait(pe, h_made, n.times(FC, f + 1 - FC))
                    for which, done in ((GATE, gate_done), (UP, up_done)):
                        hi, lo = piece(e_hi[par], which), piece(e_lo[par], which)
                        i = 0
                        for c in range(C):
                            for a, b in PASSES:
                                ins = pe.matmul(gu_ps[f][:, which, :], (hi, lo)[a][:, c, f * P:(f + 1) * P],
                                                (xt_hi, xt_lo)[b][:, blk, c, :], start=(i == 0), stop=(i == len(PASSES) * C - 1))
                                i += 1
                        ins.then_inc(done, 1)

            def down(n, free=None):
                e = n.over(NB)
                par, hp = e.parity(), n.parity()
                if n.k % NB == 0:
                    pe.wait_ge(e_lo_made, e.times(3, 3))
                pe.wait_ge(h_hi_made, n.times(FC, FC))
                pe.wait_ge(h_lo_made, n.times(FC, FC))
                hi, lo = piece(e_hi[par], DOWN), piece(e_lo[par], DOWN)
                wait(pe, added, n.times(BT))
                for t in range(BT):
                    if free is not None:
                        pe.wait_ge(e_xt_lo_made, BT * free)
                        pe.wait_ge(scale_made, free)
                    i = 0
                    for f in range(FC):
                        for a, b in PASSES:
                            ins = pe.matmul(dn_ps[t][:], (h_hi, h_lo)[a][hp][:, f, t * P:(t + 1) * P], (hi, lo)[b][:, f, :],
                                            start=(i == 0), stop=(i == len(PASSES) * FC - 1))
                            i += 1
                    ins.then_inc(down_done, 1)

            def ready_last(k):
                rows(k, BT * (STEPS - 1))
                logits(k, dn_ps[0][:], dn_ps[1][:])
                pe.wait_ge(scale_made, k + 1)

            def run(n, half):
                k = readied(n, half)
                if k is not None:
                    rows(k, BT * (n.k - 1))
                    logits(k, dn_ps[0][:], dn_ps[1][:])
                if follows(n):
                    gate_up(n + 1)
                down(n, None if k is None else k + 1)

            for k in range(NB):
                rows(k, 0)
                logits(k, gu_ps[0][:, 0, :], gu_ps[0][:, 1, :])
            pe.wait_ge(scale_made, NB)
            gate_up(At(0, TURN, 0))
            steps(pe, run, ready_last)


def kernel(**inputs):
    import numpy as np
    import concourse.bacc as bacc
    from concourse.bass_utils import run_bass_kernel_spmd

    a = {k: np.asarray(v) for k, v in inputs.items()}
    lay = np.ascontiguousarray

    def with_shared(experts_w, shared, axis):
        parts = np.split(shared, 2, axis=axis)
        return np.concatenate([experts_w, np.stack(parts)])

    arrays = {
        "x": a["x"].reshape(B * S, D),
        "ctx_t": lay(a["ctx_1024"].reshape(B * S, D).T),
        "g_xattn": a["g_xattn"],
        "g_ffn": a["g_ffn"],
        "wq_t": lay(a["L0_xattn_Wq"].T),
        "wk_t": lay(a["L0_xattn_Wk"].T),
        "wv_t": lay(a["L0_xattn_Wv"].T),
        "wo_t": lay(a["L0_xattn_Wo"].T),
        "bo": a["L0_xattn_bo"],
        "router": a["L0_ffn_router_w"],
        "w_gate": with_shared(a["L0_ffn_w_gate"], a["L0_ffn_ws_gate"], 1),
        "w_up": with_shared(a["L0_ffn_w_up"], a["L0_ffn_ws_up"], 1),
        "w_down": with_shared(a["L0_ffn_w_down"], a["L0_ffn_ws_down"], 0),
    }
    nc = bacc.Bacc("TRN2", target_bir_lowering=False, num_devices=1)
    aps = {k: nc.dram_tensor(f"in_{k}", v.shape, mybir.dt.from_np(v.dtype), kind="ExternalInput").ap() for k, v in arrays.items()}
    out = nc.dram_tensor("out_0", (B * S, D), F32, kind="ExternalOutput").ap()
    gated_block(nc, **aps, out=out)
    result = run_bass_kernel_spmd(nc, [{f"in_{k}": v for k, v in arrays.items()}], core_ids=[0])
    return result.results[0]["out_0"].reshape(B, S, D)
```

```python
from contextlib import ExitStack
from typing import Callable, NamedTuple

import concourse.bass as bass
from concourse import mybir

F32 = mybir.dt.float32
F32R = mybir.dt.float32r
F16 = mybir.dt.float16
BF16 = mybir.dt.bfloat16
I32 = mybir.dt.int32
ALU = mybir.AluOpType
ACT = mybir.ActivationFunctionType
AX = mybir.AxisListType

P = 128
B, S, D = 16, 256, 512
H = 16
DH = D // H
C = D // P
JH = P // DH
T = S // P
SCALE = float(DH) ** -0.5
EPS = 1e-5
E, F, TOP = 8, 256, 6
NE = E + 2
NEG = -3.0e38
HALF_TOKENS = B * S // 2
BLK = 512
NB = HALF_TOKENS // BLK
BT = BLK // P
FC = F // P
RSQRT_MAGIC = float(0x5F3759DF)
DMA = 16


class At:

    def __init__(self, r, step, k):
        self.r, self.step, self.k = r, step, k

    def __add__(self, k):
        return At(self.r, self.step, self.k + k)

    def parity(self):
        return self.k % 2

    def over(self, n):
        return At(self.r, self.step // n, self.k // n)

    def times(self, c, plus=0):
        fixed = c * self.k + plus
        return fixed if isinstance(self.r, int) else self.r * (c * self.step) + fixed


def wait(eng, sem, value):
    if not isinstance(value, int) or value > 0:
        eng.wait_ge(sem, value)


def row(view, index):
    v = index.times(1)
    if isinstance(v, int):
        return view[v]
    names = ["o", "p", "t", "d"][: len(view.shape)]
    rest = " ".join(names[2:])
    return view[bass.ds(v, 1)].rearrange(f"o p {rest} -> (o p) {rest}")


def newton_rsqrt(pool, chain, passed, count, y, hv, a, made):
    STEPS = 3
    for step in range(STEPS):
        for out, in0, in1 in ((a, y, y), (a, a, hv), (a, a, None), (y, y, a)):
            if in1 is None:
                pool.sem_inc(passed, 1)
                ins = pool.tensor_scalar(out, in0, 1.5, None, ALU.add)
            else:
                ins = pool.tensor_tensor(out, in0, in1, ALU.mult)
            if step == STEPS - 1 and out is y:
                ins.then_inc(made, 1)
                return
            count[0] += 1
            ins.then_inc(chain, 1)
            pool.wait_ge(chain, count[0] if isinstance(count[1], int) else count[1] + count[0])


class Start(NamedTuple):
    sync: Callable
    gpsimd: Callable
    scalar: Callable
    vector: Callable


def gated_block(nc, x, ctx_t, g_xattn, g_ffn, wq_t, wk_t, wv_t, wo_t, bo, router, w_gate, w_up, w_down, out):
    with ExitStack() as ctx:
        ident = ctx.enter_context(nc.sbuf_tensor("ident", [P, P], F32))
        gates = ctx.enter_context(nc.sbuf_tensor("gates", [P, 2], F32))
        tanh_gates = ctx.enter_context(nc.sbuf_tensor("tanh_gates", [P, 2], F32))
        x1_stored = ctx.enter_context(nc.semaphore("x1_stored"))
        x1 = nc.dram_tensor("x1_between", [B * S, D], F32, kind="Internal").ap()
        with ExitStack() as memory:
            attention_block = attention(nc, ctx, memory, x, ctx_t, g_xattn, g_ffn, wq_t, wk_t, wv_t, wo_t, bo, x1, x1_stored,
                                        ident, gates, tanh_gates)
        start, experts_block = experts(nc, ctx, x1, x1_stored, router, w_gate, w_up, w_down, out, ident, tanh_gates)
        attention_block(start)
        experts_block()


def attention(nc, ctx, memory, x, ctx_t, g_xattn, g_ffn, wq_t, wk_t, wv_t, wo_t, bo, x1, x1_stored, ident, gates, tanh_gates):
    def sb(name, shape, dt=F32):
        return memory.enter_context(nc.sbuf_tensor(name, shape, dt))

    def psum(name, shape):
        return memory.enter_context(nc.psum_tensor(name, shape, F32))

    def sem(name):
        return ctx.enter_context(nc.semaphore(name))

    WQ, WK, WV, WO = range(4)
    RAW_ORDER = (WK, WQ, WV, WO)
    HD = D // 2
    N_RAW = len(RAW_ORDER) * 2

    w_hi, w_lo = (sb(f"w_{n}", [P, 4, C, D], F32R) for n in ("hi", "lo"))

    def stacks(i):
        return sb(f"q_stack{i}", [P, H, S], F32R), sb(f"k_stack{i}", [P, H, S], F32R)

    even = stacks(0)
    x_res = sb("x_res", [P, T, D])
    with ExitStack() as weights_first:
        raw = [weights_first.enter_context(nc.sbuf_tensor(f"raw{n}", [P, C, HD], F32))[:] for n in range(N_RAW)]
    odd = stacks(1)
    q_stack, k_stack = zip(even, odd)
    x_in = sb("x_in", [P, T, D])
    c_in = sb("c_in", [P, C, S])
    c_hi, c_lo = sb("c_hi", [P, C, S], F32R), sb("c_lo", [P, C, S], F32R)
    t_hi, t_lo = sb("t_hi", [P, C, S], F32R), sb("t_lo", [P, C, S], F32R)
    q_hi, q_lo = sb("q_hi", [P, C, S], F32R), sb("q_lo", [P, C, S], F32R)
    k_hi, k_lo = sb("k_hi", [P, C, S], F32R), sb("k_lo", [P, C, S], F32R)
    v_parts = [sb(f"v_parts{i}", [P, T, 3, D], BF16) for i in range(2)]
    v_rest = sb("v_rest", [P, D])
    RING = 4
    probs = [sb(f"probs{i}", [P, 3 * P]) for i in range(RING)]
    pt_hi = [sb(f"pt_hi{i}", [P, 3 * P], F16) for i in range(2)]
    pt_lo = [sb(f"pt_lo{i}", [P, 3 * P], F16) for i in range(2)]
    Y_LATE = 2
    y = sb("y", [P, Y_LATE + 1, T, D // 2])
    y_sum = sb("y_sum", [P, T * JH, DH])
    mask = sb("mask", [P, 2 * P])
    bias = sb("bias", [P, D])
    neg_max = sb("neg_max", [P, H, T])
    row_sum = sb("row_sum", [P, H, T])
    row_inv = sb("row_inv", [P, JH, T])
    stats, mv = sb("stats", [P, T, 6]), sb("mv", [P, T, 2])
    var_eps, shifted = sb("var_eps", [P, T]), sb("shifted", [P, T], I32)
    half_var, rstd, newton = sb("half_var", [P, T]), sb("rstd", [P, T]), sb("newton", [P, T])

    bank = [psum(f"bank{i}", [P, D]) for i in range(2)]
    sc_ps = [psum(f"scores{i}", [P, T, S]) for i in range(2)]
    pt_ps = [psum(f"probs_t{i}", [P, D]) for i in range(2)]
    y_ps = [psum(f"y{i}", [P, T, JH, 2, DH]) for i in range(2)]

    raw_loaded = [sem(f"raw_loaded{i}") for i in range(N_RAW)]
    small_loaded = sem("small_loaded")
    x_loaded, c_loaded, res_loaded = sem("x_loaded"), sem("c_loaded"), sem("res_loaded")
    stacked = [[sem(f"stacked{i}_{j}") for j in range(JH)] for i in range(2)]
    ident_made, mask_made, bias_made = sem("ident_made"), sem("mask_made"), sem("bias_made")
    pool_chain, rstd_made, c_lo_made, v3_made = sem("pool_chain"), sem("rstd_made"), sem("c_lo_made"), sem("v3_made")
    res_made = sem("res_made")
    pool_passed, dve_passed, sp_passed = sem("pool_passed"), sem("dve_passed"), sem("sp_passed")
    w_hi_made, tanh_made, c_hi_made = sem("w_hi_made"), sem("tanh_made"), sem("c_hi_made")
    xt_hi_made, q_hi_made, k_hi_made = sem("xt_hi_made"), sem("q_hi_made"), sem("k_hi_made")
    v1_made, v2_made, yt_hi_made = sem("v1_made"), sem("v2_made"), sem("yt_hi_made")
    probs_made, pt_hi_made = sem("probs_made"), sem("pt_hi_made")
    w_lo_made, guess_made, norm_chain = sem("w_lo_made"), sem("guess_made"), sem("norm_chain")
    xn_made, group_chain = sem("xn_made"), sem("group_chain")
    xt_lo_made, q_lo_made, k_lo_made = sem("xt_lo_made"), sem("q_lo_made"), sem("k_lo_made")
    v_rest_made, yt_lo_made, x1_made = sem("v_rest_made"), sem("yt_lo_made"), sem("x1_made")
    max_made, pt_lo_made, y_made = sem("max_made"), sem("pt_lo_made"), sem("y_made")
    xt_done, q_done, k_done, v_done = sem("xt_done"), sem("q_done"), sem("k_done"), sem("v_done")
    yt_done, o_done = sem("yt_done"), sem("o_done")
    scores_done, pt_done, pv_done = sem("scores_done"), sem("pt_done"), sem("pv_done")

    x_v = x.rearrange("(b t p) d -> b p t d", p=P, t=T)
    x1_v = x1.rearrange("(b t p) d -> b p t d", p=P, t=T)
    c_v = ctx_t.rearrange("(c p) (b t) -> b p c t", p=P, b=B)
    w_v = [w.rearrange("(c p) o -> p c o", p=P) for w in (wq_t, wk_t, wv_t, wo_t)]
    STACK_DMAS = 2 * 3
    PAIR = 2

    FIRST, PAIRS = 3, 5

    def iterations(eng, run):
        for i in range(-1, FIRST):
            run(At(0, 2, i))
        with eng.Fori(0, PAIRS) as r:
            for u in range(2):
                run(At(r, 2, FIRST + u))
        for i in range(FIRST + 2 * PAIRS, B + 1):
            run(At(0, 2, i))

    def has(i, ahead):
        return not isinstance(i.r, int) or 0 <= i.k + ahead < B

    def lagging(i, s, lag):
        back = s < lag
        if not has(i, -back):
            return None
        return i + (-1 if back else 0), (s - lag) % H

    TR_LAG, PV_LAG = 2, 4
    GROUP_LAG = PV_LAG + JH
    BANK_A, BANK_B = 0, 1
    K_SLOTS, K_EVAC = (0, 1, 2, 3), (2, 4)
    X_SLOTS, X_EVAC, X_BANKS = (0, 2), (1, 3), (BANK_B, BANK_A)
    Q_SLOTS, Q_EVAC = (4, 5, 6, 7), (6, 8)
    V_SLOTS, V_EVAC, V_SPLIT = ((8, 9), (10, 11)), (10, 12), (11, 13)
    Y_SLOTS, Y_EVAC, Y_BANKS = (8, 10), (9, 11), (BANK_B, BANK_A)
    O_SLOTS, O_EVAC = ((12, 13), (14, 15)), (14, 15)
    RES_SLOT, LN_SLOT, C_SLOT, XN_SLOT = 6, 5, 12, 13
    START_SLOT = 12

    def is_last(i):
        return isinstance(i.r, int) and i.k == B - 1

    def is_end(i):
        return isinstance(i.r, int) and i.k == B

    def weights_at(i, s):
        return {0: (2, 3), 3: (4, 5), 7: (6, 7)}.get(s, ()) if isinstance(i.r, int) and i.k == -1 else ()

    def build(start):
        with nc.Block() as block:
            @block.sync
            def _(sp):
                sp.dma_start(c_in[:], c_v[0]).then_inc(c_loaded, DMA)
                sp.dma_start(x_in[:], x_v[0]).then_inc(x_loaded, DMA)
                for n in range(N_RAW):
                    src = w_v[RAW_ORDER[n // 2]][:, :, (n % 2) * HD:(n % 2 + 1) * HD]
                    sp.dma_start(raw[n], src).then_inc(raw_loaded[n], DMA)
                    if n == 1:
                        sp.dma_start(gates[:, 0:1], g_xattn.partition_broadcast(P)).then_inc(small_loaded, DMA)
                        sp.dma_start(gates[:, 1:2], g_ffn.partition_broadcast(P)).then_inc(small_loaded, DMA)
                        sp.dma_start(bias[:], bo.partition_broadcast(P)).then_inc(small_loaded, DMA)
                sp.wait_ge(c_lo_made, 1)
                sp.dma_start(c_in[:], c_v[1]).then_inc(c_loaded, DMA)

                def stack(dst, j, group, src):
                    lo, hi = group * DH, (group + 1) * DH
                    return sp.dma_start(dst[lo:hi, j:H:JH, :].bitcast(F32), src[j * DH:(j + 1) * DH].bitcast(F32))

                def run(i):
                    n, o, ln, far = i + 1, i + -1, i + 2, i + 3
                    par = n.parity()
                    if has(i, -1):
                        wait(sp, x1_stored, o.times(DMA))
                        sp.dma_start(x_res[:], row(x_v, o)).then_inc(res_loaded, DMA)
                    if is_last(i):
                        sp.wait_ge(scores_done, H * (B - 1))
                        sp.wait_ge(x1_stored, BLK // S * DMA)
                        start.sync(sp)
                    if has(i, 2):
                        sp.wait_ge(xt_done, ln.times(T))
                        sp.dma_start(x_in[:], row(x_v, ln)).then_inc(x_loaded, DMA)
                    if has(i, 1):
                        if isinstance(i.r, int) and i.k == 0:
                            sp.wait_ge(w_lo_made, N_RAW)
                        wait(sp, scores_done, n.times(H, -H))
                        sp.sem_inc(sp_passed, 1)
                        sp.wait_ge(k_lo_made, n.times(2, 2))
                        for j in range(JH):
                            stack(k_stack[par], j, 0, k_hi).then_inc(stacked[par][j], DMA)
                            stack(k_stack[par], j, 1, k_hi).then_inc(stacked[par][j], DMA)
                            stack(k_stack[par], j, 2, k_lo).then_inc(stacked[par][j], DMA)
                    if has(i, 1):
                        sp.wait_ge(q_lo_made, n.times(2, 2))
                        for j in range(JH):
                            stack(q_stack[par], j, 0, q_hi).then_inc(stacked[par][j], DMA)
                            stack(q_stack[par], j, 1, q_lo).then_inc(stacked[par][j], DMA)
                            stack(q_stack[par], j, 2, q_hi).then_inc(stacked[par][j], DMA)
                    if has(i, 3):
                        sp.wait_ge(c_lo_made, far.times(1))
                        sp.dma_start(c_in[:], row(c_v, far)).then_inc(c_loaded, DMA)
                    if has(i, -1):
                        sp.wait_ge(x1_made, o.times(T, T))
                        sp.dma_start(row(x1_v, o), x_res[:]).then_inc(x1_stored, DMA)

                iterations(sp, run)

            @block.gpsimd
            def _(pool):
                pool.memset(ident[:], 0.0).then_inc(pool_chain, 1)
                pool.memset(mask[:], 0.0).then_inc(pool_chain, 1)
                pool.wait_ge(pool_chain, 2)
                pool.affine_select(out=ident[:], in_=ident[:], compare_op=ALU.not_equal, fill=1.0, base=0,
                                   pattern=[[-1, P]], channel_multiplier=1).then_inc(ident_made, 1)
                pool.affine_select(out=mask[:, P:], in_=mask[:, P:], compare_op=ALU.is_ge, fill=NEG, base=0,
                                   pattern=[[-1, P]], channel_multiplier=1).then_inc(mask_made, 1)
                NEWTON = 11

                def inverse_std(ln):
                    pool.wait_ge(guess_made, ln.times(1, 1))
                    first = 2 + NEWTON * ln.k
                    base = 0 if isinstance(ln.r, int) else ln.r * (NEWTON * ln.step)
                    newton_rsqrt(pool, pool_chain, pool_passed, [first, base], rstd[:], half_var[:], newton[:], rstd_made)

                def context_lo(n):
                    pool.wait_ge(c_hi_made, n.times(1, 1))
                    pool.tensor_tensor(c_lo[:], c_in[:], c_hi[:].bitcast(F32), ALU.subtract).then_inc(c_lo_made, 1)

                def run(i):
                    n, o, ln = i + 1, i + -1, i + 2
                    for s in range(H):
                        if s in V_SPLIT and has(i, 1):
                            t, parts = V_SPLIT.index(s), v_parts[n.parity()]
                            pool.wait_ge(v2_made, n.times(T, t + 1))
                            pool.tensor_tensor(parts[:, t, 2, :], v_rest[:], parts[:, t, 1, :], ALU.subtract).then_inc(v3_made, 1)
                        if s == C_SLOT and has(i, 2):
                            context_lo(ln)
                        if s == RES_SLOT and has(i, -1):
                            pool.wait_ge(res_loaded, o.times(DMA, DMA))
                            for t in range(T):
                                pool.tensor_tensor(x_res[:, t, :], x_res[:, t, :], bias[:], ALU.add).then_inc(res_made, 1)
                        if s == LN_SLOT and has(i, 2):
                            inverse_std(ln)
                        if is_end(i) and s == START_SLOT:
                            start.gpsimd(pool)

                context_lo(At(0, 2, 0))
                inverse_std(At(0, 2, 0))
                pool.wait_ge(small_loaded, 3 * DMA)
                pool.wait_ge(tanh_made, 1)
                pool.tensor_scalar(bias[:], bias[:], tanh_gates[:, 0:1], None, ALU.mult).then_inc(bias_made, 1)
                pool.wait_ge(bias_made, 1)
                iterations(pool, run)

            @block.scalar
            def _(act):
                def context_hi(n):
                    act.wait_ge(c_loaded, n.times(DMA, DMA))
                    wait(act, v_done, n.times(T))
                    act.copy(c_hi[:], c_in[:]).then_inc(c_hi_made, 1)

                context_hi(At(0, 2, 0))
                def weights_hi(n):
                    act.wait_ge(raw_loaded[n], DMA)
                    act.copy(w_hi[:, RAW_ORDER[n // 2], :, (n % 2) * HD:(n % 2 + 1) * HD], raw[n]).then_inc(w_hi_made, 1)

                weights_hi(0)
                weights_hi(1)
                act.wait_ge(small_loaded, 3 * DMA)
                act.activation(tanh_gates[:], gates[:], ACT.Tanh).then_inc(tanh_made, 1)

                def rows_hi(t, b, made):
                    act.copy(t_hi[:, :, t * P:(t + 1) * P], bank[b][:].rearrange("p (c t) -> p c t", c=C)).then_inc(made, 1)

                def run(i):
                    n, o, ln = i + 1, i + -1, i + 2
                    for s in range(H):
                        if has(i, 1):
                            if s in V_EVAC:
                                t, parts = V_EVAC.index(s), v_parts[n.parity()]
                                act.wait_ge(v_done, n.times(T, t + 1))
                                if t == 0:
                                    wait(act, pv_done, n.times(H, -H))
                                act.copy(parts[:, t, 0, :], bank[t][:]).then_inc(v1_made, 1)
                            if s in V_SPLIT:
                                t, parts = V_SPLIT.index(s), v_parts[n.parity()]
                                act.wait_ge(v_rest_made, n.times(T, t + 1))
                                act.copy(parts[:, t, 1, :], v_rest[:]).then_inc(v2_made, 1)
                            if s in X_EVAC:
                                t = X_EVAC.index(s)
                                act.wait_ge(xt_done, n.times(T, t + 1))
                                if t == 0:
                                    wait(act, q_done, n.times(2))
                                    wait(act, o_done, n.times(T, -2 * T))
                                rows_hi(t, X_BANKS[t], xt_hi_made)
                            for slots, hi, done, made in ((Q_EVAC, q_hi, q_done, q_hi_made), (K_EVAC, k_hi, k_done, k_hi_made)):
                                if s in slots:
                                    u = slots.index(s)
                                    act.wait_ge(done, n.times(2, u + 1))
                                    if u == 0 and (not isinstance(n.r, int) or n.k > 0):
                                        m = n + -1
                                        for j in range(JH):
                                            act.wait_ge(stacked[m.parity()][j], m.over(2).times(STACK_DMAS * DMA, STACK_DMAS * DMA))
                                    act.copy(hi[:, PAIR * u:PAIR * (u + 1), :],
                                             bank[u][:].rearrange("p (m t) -> p m t", m=PAIR)).then_inc(made, 1)
                        if s in Y_EVAC and has(i, -1):
                            t = Y_EVAC.index(s)
                            act.wait_ge(yt_done, o.times(T, t + 1))
                            if t == 0 and has(i, 1):
                                act.wait_ge(q_done, n.times(2, 2))
                            elif t == 0:
                                wait(act, o_done, o.times(T))
                            rows_hi(t, Y_BANKS[t], yt_hi_made)
                        if (bh := lagging(i, s, TR_LAG)):
                            b, h = bh
                            act.wait_ge(pt_done, b.times(H, h + 1))
                            wait(act, pv_done, b.times(H, h - 1))
                            act.copy(pt_hi[h % 2][:], pt_ps[h % 2][:, 0:3 * P]).then_inc(pt_hi_made, 1)
                        if has(i, 0):
                            act.wait_ge(max_made, i.times(H, s + 1))
                            p = probs[s % RING]
                            act.activation(p[:, 0:P], p[:, 0:P], ACT.Exp, bias=neg_max[:, s, 0:1],
                                           scale=-1.0, accum_out=row_sum[:, s, 0:1])
                            act.activation(p[:, P:], p[:, P:], ACT.Exp, bias=neg_max[:, s, 1:2],
                                           scale=-1.0, accum_out=row_sum[:, s, 1:2]).then_inc(probs_made, 1)
                        if s == C_SLOT and has(i, 2):
                            context_hi(ln)
                        for m in weights_at(i, s):
                            weights_hi(m)
                        if is_end(i) and s == START_SLOT:
                            act.wait_ge(k_done, 2 * B)
                            act.wait_ge(q_done, 2 * B)
                            act.wait_ge(v_done, T * B)
                            start.scalar(act)

                iterations(act, run)

            @block.vector
            def _(dve):
                NORM_STEPS = 2 * T + 2
                PER_GROUP = 2

                def statistics(ln):
                    dve.wait_ge(x_loaded, ln.times(DMA, DMA))
                    for t in range(T):
                        dve.bn_stats(stats[:, t, :], x_in[:, t, :]).then_inc(norm_chain, 1)
                    dve.wait_ge(norm_chain, ln.times(NORM_STEPS, T))
                    wait(dve, xn_made, ln.times(T))
                    dve.sem_inc(dve_passed, 1)
                    for t in range(T):
                        dve.bn_aggr(mv[:, t, :], stats[:, t, :]).then_inc(norm_chain, 1)
                    dve.wait_ge(norm_chain, ln.times(NORM_STEPS, 2 * T))
                    dve.tensor_scalar(var_eps[:], mv[:, :, 1], EPS, None, ALU.add).then_inc(norm_chain, 1)
                    dve.wait_ge(norm_chain, ln.times(NORM_STEPS, 2 * T + 1))
                    dve.tensor_scalar(shifted[:], var_eps[:].bitcast(I32), 1, None,
                                      ALU.logical_shift_right).then_inc(norm_chain, 1)
                    dve.tensor_scalar(half_var[:], var_eps[:], -0.5, None, ALU.mult)
                    dve.wait_ge(norm_chain, ln.times(NORM_STEPS, 2 * T + 2))
                    dve.tensor_scalar(rstd[:].bitcast(I32), shifted[:], -1.0, RSQRT_MAGIC, ALU.mult,
                                      ALU.add).then_inc(guess_made, 1)

                def normalise(ln):
                    dve.wait_ge(rstd_made, ln.times(1, 1))
                    for t in range(T):
                        dve.tensor_scalar(x_in[:, t, :], x_in[:, t, :], mv[:, t, 0:1], rstd[:, t:t + 1],
                                          ALU.subtract, ALU.mult).then_inc(xn_made, 1)

                statistics(At(0, 2, 0))
                def weights_lo(n):
                    dve.wait_ge(w_hi_made, n + 1)
                    part = (slice(None), RAW_ORDER[n // 2], slice(None), slice((n % 2) * HD, (n % 2 + 1) * HD))
                    dve.tensor_tensor(w_lo[part], raw[n], w_hi[part].bitcast(F32), ALU.subtract).then_inc(w_lo_made, 1)

                weights_lo(0)
                weights_lo(1)
                normalise(At(0, 2, 0))
                dve.wait_ge(mask_made, 1)

                def rows_lo(t, b, made):
                    part = slice(t * P, (t + 1) * P)
                    dve.tensor_tensor(t_lo[:, :, part], bank[b][:].rearrange("p (c t) -> p c t", c=C),
                                      t_hi[:, :, part].bitcast(F32), ALU.subtract).then_inc(made, 1)

                def close_group(b, g):
                    steps = PER_GROUP * (H // JH)
                    first, heads = PER_GROUP * g, slice(JH * g, JH * (g + 1))
                    dve.wait_ge(pv_done, b.times(H, JH * (g + 1)))
                    if g in (0, 2):
                        wait(dve, yt_done, b.times(T, -T if g == 0 else 0))
                    dve.reciprocal(row_inv[:], row_sum[:, heads, :]).then_inc(group_chain, 1)
                    dve.tensor_reduce(y_sum[:], y_ps[g % 2][:].rearrange("p t h x d -> p (t h) d x"), AX.X,
                                      ALU.add).then_inc(group_chain, 1)
                    dve.wait_ge(group_chain, b.times(steps, first + PER_GROUP))
                    part, at = (b.parity(), g * P) if g < 2 else (Y_LATE, (g - 2) * P)
                    dve.tensor_tensor(y[:, part, :, at:at + P].rearrange("p t (h d) -> p t h d", d=DH),
                                      y_sum[:].rearrange("p (t h) d -> p t h d", t=T),
                                      row_inv[:].rearrange("p h t -> p t h").unsqueeze(3).to_broadcast([P, T, JH, DH]),
                                      ALU.mult).then_inc(y_made, 1)

                def residual(o, t):
                    dve.wait_ge(o_done, o.times(T, t + 1))
                    dve.wait_ge(res_made, o.times(T, t + 1))
                    dve.scalar_tensor_tensor(out=x_res[:, t, :], in0=bank[t][:], scalar=tanh_gates[:, 0:1],
                                             in1=x_res[:, t, :], op0=ALU.mult, op1=ALU.add).then_inc(x1_made, 1)

                def run(i):
                    n, o, ln = i + 1, i + -1, i + 2
                    for s in range(H):
                        if has(i, 0):
                            dve.wait_ge(scores_done, i.times(H, s + 1))
                            wait(dve, pt_done, i.times(H, s - RING + 1))
                            dve.sem_inc(dve_passed, 1)
                            p = probs[s % RING]
                            for t in range(T):
                                keys = slice(0, P * (t + 1))
                                dst = p[:, 0:P] if t == 0 else p[:, P:]
                                ins = dve.tensor_tensor_reduce(dst, sc_ps[s % 2][:, t, keys], mask[:, P * (1 - t):], -SCALE, -NEG,
                                                               ALU.add, ALU.min, neg_max[:, s, t:t + 1])
                            ins.then_inc(max_made, 1)
                        if has(i, 1):
                            if s in V_EVAC:
                                t = V_EVAC.index(s)
                                dve.wait_ge(v1_made, n.times(T, t + 1))
                                wait(dve, v3_made, n.times(T, t))
                                dve.tensor_tensor(v_rest[:], bank[t][:], v_parts[n.parity()][:, t, 0, :],
                                                  ALU.subtract).then_inc(v_rest_made, 1)
                            if s in X_EVAC:
                                t = X_EVAC.index(s)
                                dve.wait_ge(xt_hi_made, n.times(T, t + 1))
                                rows_lo(t, X_BANKS[t], xt_lo_made)
                            for slots, hi, lo, hi_made, made in ((Q_EVAC, q_hi, q_lo, q_hi_made, q_lo_made),
                                                                 (K_EVAC, k_hi, k_lo, k_hi_made, k_lo_made)):
                                if s in slots:
                                    u = slots.index(s)
                                    part = slice(PAIR * u, PAIR * (u + 1))
                                    dve.wait_ge(hi_made, n.times(2, u + 1))
                                    dve.tensor_tensor(lo[:, part, :], bank[u][:].rearrange("p (m t) -> p m t", m=PAIR),
                                                      hi[:, part, :].bitcast(F32), ALU.subtract).then_inc(made, 1)
                        if has(i, -1):
                            if s in Y_EVAC:
                                t = Y_EVAC.index(s)
                                dve.wait_ge(yt_hi_made, o.times(T, t + 1))
                                rows_lo(t, Y_BANKS[t], yt_lo_made)
                            if s == O_EVAC[0]:
                                residual(o, 0)
                        if (bh := lagging(i, s, TR_LAG)):
                            b, h = bh
                            dve.wait_ge(pt_hi_made, b.times(H, h + 1))
                            dve.tensor_tensor(pt_lo[h % 2][:], pt_ps[h % 2][:, 0:3 * P], pt_hi[h % 2][:],
                                              ALU.subtract).then_inc(pt_lo_made, 1)
                        if (bh := lagging(i, s, GROUP_LAG)) and bh[1] % JH == 0:
                            close_group(bh[0], bh[1] // JH)
                        for m in weights_at(i, s):
                            weights_lo(m)
                        if is_end(i) and s == START_SLOT:
                            start.vector(dve)
                        if s == LN_SLOT and has(i, 2):
                            statistics(ln)
                        if s == XN_SLOT and has(i, 2):
                            normalise(ln)
                        if s == O_EVAC[1] and has(i, -1):
                            residual(o, 1)

                iterations(dve, run)

            @block.tensor
            def _(pe):
                pe.wait_ge(ident_made, 1)
                PASSES = ((0, 0), (1, 0), (0, 1))
                HALF_CHUNKS = (range(0, C // 2), range(C // 2, C))

                def transpose_rows(chunk, dst):
                    for c in range(C):
                        ins = pe.transpose(dst[:, c * P:(c + 1) * P], chunk(c), ident[:])
                    return ins

                def y_chunk(b, t, c):
                    return y[:, b.parity() if c < 2 else Y_LATE, t, c % 2 * P:(c % 2 + 1) * P]

                def three_pass(dst, stationary, moving, chunks=range(C)):
                    for c in chunks:
                        for k, (a, b) in enumerate(PASSES):
                            ins = pe.matmul(dst, stationary[a](c), moving[b](c), start=(c == 0 and k == 0),
                                            stop=(c == C - 1 and k == len(PASSES) - 1))
                    return ins

                def weight(mat, lo=0, hi=D):
                    return lambda c: w_hi[:, mat, c, lo:hi], lambda c: w_lo[:, mat, c, lo:hi]

                def rows(hi, lo, part=slice(0, S)):
                    return lambda c: hi[:, c, part], lambda c: lo[:, c, part]

                def tile(t):
                    return slice(t * P, (t + 1) * P)

                def split(mat, first, halves=2):
                    wait(pe, w_lo_made, 2 * RAW_ORDER.index(mat) + halves if first else 0)

                def project(m, mat, src, done):
                    ins = three_pass(bank[m // PAIR][:, (m % PAIR) * S:(m % PAIR + 1) * S],
                                     weight(mat, m * P, (m + 1) * P), src)
                    if m % PAIR == PAIR - 1:
                        ins.then_inc(done, 1)

                def units(i, s):
                    n, o = i + 1, i + -1
                    first = isinstance(n.r, int) and n.k == 0
                    if has(i, 1):
                        if s in K_SLOTS:
                            m = K_SLOTS.index(s)
                            if m == 0:
                                pe.wait_ge(c_lo_made, n.times(1, 1))
                                split(WK, first, 1)
                                wait(pe, x1_made, n.times(T, 1 - 3 * T))
                            elif m == PAIR:
                                split(WK, first)
                                pe.wait_ge(xt_lo_made, n.times(T, 1))
                            project(m, WK, rows(c_hi, c_lo), k_done)
                        if s in X_SLOTS:
                            t = X_SLOTS.index(s)
                            pe.wait_ge(xn_made, n.times(T, t + 1))
                            if t == 0:
                                wait(pe, x1_made, n.times(T, 2 - 3 * T))
                            else:
                                pe.wait_ge(k_lo_made, n.times(2, 1))
                            transpose_rows(lambda c: x_in[:, t, c * P:(c + 1) * P], bank[X_BANKS[t]]).then_inc(xt_done, 1)
                        if s in Q_SLOTS:
                            m = Q_SLOTS.index(s)
                            if m == 0:
                                split(WQ, first, 1)
                                pe.wait_ge(xt_lo_made, n.times(T, T))
                            elif m == PAIR:
                                split(WQ, first)
                                pe.wait_ge(k_lo_made, n.times(2, 2))
                            project(m, WQ, rows(t_hi, t_lo), q_done)
                        for t in range(T):
                            if s in V_SLOTS[t]:
                                half = V_SLOTS[t].index(s)
                                if half == 0 and t == 0:
                                    split(WV, first)
                                    pe.wait_ge(q_lo_made, n.times(2, 1))
                                elif half == 0 and has(i, -1):
                                    pe.wait_ge(yt_lo_made, o.times(T, 1))
                                elif half == 0:
                                    pe.wait_ge(q_lo_made, n.times(2, 2))
                                ins = three_pass(bank[t][:], rows(c_hi, c_lo, tile(t)), weight(WV), HALF_CHUNKS[half])
                                if half == 1:
                                    ins.then_inc(v_done, 1)
                    if has(i, -1):
                        if s in Y_SLOTS:
                            t = Y_SLOTS.index(s)
                            if t == 0:
                                pe.wait_ge(y_made, o.times(H // JH, H // JH))
                            if has(i, 1) and t == 0:
                                pe.wait_ge(q_lo_made, n.times(2, 2))
                            elif has(i, 1):
                                pe.wait_ge(v_rest_made, n.times(T, 1))
                            else:
                                wait(pe, x1_made, o.times(T, (0, 1 - T)[t]))
                            transpose_rows(lambda c: y_chunk(o, t, c), bank[Y_BANKS[t]]).then_inc(yt_done, 1)
                        for t in range(T):
                            if s in O_SLOTS[t]:
                                half = O_SLOTS[t].index(s)
                                if half == 0 and t == 0:
                                    split(WO, isinstance(o.r, int) and o.k == 0)
                                    pe.wait_ge(yt_lo_made, o.times(T, T))
                                elif half == 0 and has(i, 1):
                                    pe.wait_ge(v_rest_made, n.times(T, T))
                                ins = three_pass(bank[t][:], rows(t_hi, t_lo, tile(t)), weight(WO), HALF_CHUNKS[half])
                                if half == 1:
                                    ins.then_inc(o_done, 1)

                def run(i):
                    for s in range(H):
                        if has(i, 0):
                            par = i.parity()
                            if s < JH:
                                pe.wait_ge(stacked[par][s], i.over(2).times(STACK_DMAS * DMA, STACK_DMAS * DMA))
                            wait(pe, max_made, i.times(H, s - 1))
                            pairs = slice(0, 3 * DH)
                            for t in range(T):
                                ins = pe.matmul(sc_ps[s % 2][:, t, :], q_stack[par][pairs, s, tile(t)],
                                                k_stack[par][pairs, s, :], start=True, stop=True)
                            ins.then_inc(scores_done, 1)
                        if (bh := lagging(i, s, PV_LAG)):
                            b, h = bh
                            g, hg, v = h // JH, h % JH, v_parts[b.parity()]
                            if h == 0:
                                pe.wait_ge(v3_made, b.times(T, T))
                            if hg == 0:
                                wait(pe, y_made, b.times(H // JH, g - 1))
                            pe.wait_ge(pt_lo_made, b.times(H, h + 1))
                            col = slice(h * DH, (h + 1) * DH)
                            for t, blocks in ((0, ((0, 0),)), (1, ((1, 0), (2, 1)))):
                                for k, (blk, key) in enumerate(blocks):
                                    last = k == len(blocks) - 1
                                    dst = y_ps[g % 2][:, t, hg]
                                    pe.matmul(dst, pt_hi[h % 2][:, tile(blk)], v[:, key, 0:2, col], start=(k == 0), stop=False)
                                    pe.matmul(dst[:, 1], pt_hi[h % 2][:, tile(blk)], v[:, key, 2, col], start=False, stop=False)
                                    ins = pe.matmul(dst, pt_lo[h % 2][:, tile(blk)], v[:, key, 0:2, col], start=False, stop=last)
                            ins.then_inc(pv_done, 1)
                        if (bh := lagging(i, s, TR_LAG)):
                            b, h = bh
                            pe.wait_ge(probs_made, b.times(H, h + 1))
                            wait(pe, pt_lo_made, b.times(H, h - 1))
                            for k in range(3):
                                ins = pe.transpose(pt_ps[h % 2][:, tile(k)], probs[h % RING][:, tile(k)], ident[:])
                            ins.then_inc(pt_done, 1)
                        units(i, s)

                iterations(pe, run)

    return build


def experts(nc, ctx, x1, x1_stored, router, w_gate, w_up, w_down, out, ident, tanh_gates):
    def sb(name, shape, dt=F32):
        return ctx.enter_context(nc.sbuf_tensor(name, shape, dt))

    def sem(name):
        return ctx.enter_context(nc.semaphore(name))

    HALVES, U = 2, 2
    STEPS = NE * NB
    TURN = U * NB
    WP = C * F
    GATE, UP, DOWN = range(3)

    SLOTS = NB + 1
    e_hi = [sb(f"e_hi{i}", [P, 3, WP], F32R) for i in range(2)]
    acc_2 = sb("acc2", [P, BT, D])
    e_lo = [sb(f"e_lo{i}", [P, 3, WP], F32R) for i in range(2)]
    acc_1 = sb("acc1", [P, BT, D])
    w_raw = sb("w_raw", [P, 3, WP])
    acc_0 = sb("acc0", [P, BT, D])
    xn = [sb(f"xn{i}", [P, D]) for i in range(BT)]
    r_w, r_parts = sb("router_w", [P, C, E]), sb("r_parts", [P, C, 2, E], F32R)
    fold = sb("fold", [2 * E, E])
    before = sb("before", [P, E, E])
    stats, mv = sb("norm_stats", [P, BT, 6]), sb("norm_mv", [P, BT, 2])
    var_eps, shifted = sb("norm_var_eps", [P, BT]), sb("norm_shifted", [P, BT], I32)
    half_var, rstd, newton = sb("norm_half_var", [P, BT]), sb("norm_rstd", [P, BT]), sb("norm_newton", [P, BT])
    offset = sb("norm_offset", [P, BT])
    acc = [acc_0, acc_1, acc_2] + [sb(f"acc{i}", [P, BT, D]) for i in range(3, SLOTS)]
    xt_hi, xt_lo = sb("xt_hi", [P, NB, C, BLK], F32R), sb("xt_lo", [P, NB, C, BLK], F32R)
    h_hi = [sb(f"h_hi{i}", [P, FC, BLK], F32R) for i in range(2)]
    h_lo = [sb(f"h_lo{i}", [P, FC, BLK], F32R) for i in range(2)]
    silu = [sb(f"silu{i}", [P, BLK]) for i in range(FC)]
    h = [sb(f"h{i}", [P, BLK]) for i in range(FC)]
    logits_t = sb("logits_t", [2 * E, BLK])
    top, total, inverse = sb("top", [P, BT]), sb("total", [P, BT]), sb("inverse", [P, BT])
    shift, weights, share = sb("shift", [P, BT, E]), sb("weights", [P, BT, E]), sb("share", [P, BT, E])
    rank = sb("rank", [P, BT, E])
    ahead, equal = sb("ahead", [P, BT, E, E]), sb("equal", [P, BT, E, E])
    scale = sb("scale", [P, HALVES * NB, BT, NE])

    gu_ps = [ctx.enter_context(nc.psum_tensor(f"gate_up{i}", [P, 2, BLK], F32)) for i in range(FC)]
    dn_ps = [ctx.enter_context(nc.psum_tensor(f"down{i}", [P, D], F32)) for i in range(BT)]

    raw_loaded = [sem(f"e_raw_loaded{i}") for i in range(3)]
    r_loaded = sem("r_loaded")
    x1_loaded = [sem(f"x1_loaded{i}") for i in range(HALVES * NB)]
    stored = sem("stored")
    e_rstd_made, e_offset_made = sem("e_rstd_made"), sem("e_offset_made")
    e_pool_passed = sem("e_pool_passed")
    before_set, before_made, e_pool_chain, e_xn_made = sem("before_set"), sem("before_made"), sem("e_pool_chain"), sem("e_xn_made")
    silu_made, h_hi_made, e_hi_made = sem("silu_made"), sem("h_hi_made"), sem("e_hi_made")
    r_hi_made, e_xt_hi_made, logits_made, exp_made = sem("r_hi_made"), sem("e_xt_hi_made"), sem("logits_made"), sem("exp_made")
    h_made, h_lo_made, e_lo_made, added = sem("h_made"), sem("h_lo_made"), sem("e_lo_made"), sem("added")
    r_lo_made, e_guess_made, e_xt_lo_made = sem("r_lo_made"), sem("e_guess_made"), sem("e_xt_lo_made")
    shift_made, scale_made = sem("shift_made"), sem("scale_made")
    e_norm_chain, route_chain, shared_set = sem("e_norm_chain"), sem("route_chain"), sem("shared_set")
    gate_done, up_done, down_done = sem("gate_done"), sem("up_done"), sem("down_done")
    e_xt_done, logits_done, logits_back = sem("e_xt_done"), sem("logits_done"), sem("logits_back")

    x1_v = x1.rearrange("(k t p) d -> k p t d", p=P, t=BT)
    out_v = out.rearrange("(k t p) d -> k p t d", p=P, t=BT)
    g_v = w_gate.rearrange("e (c p) f -> e p c f", p=P)
    u_v = w_up.rearrange("e (c p) f -> e p c f", p=P)
    d_v = w_down.rearrange("e (f p) d -> e p f d", p=P)

    def piece(tile, which):
        part = tile[:, which, :]
        return part.rearrange("p (c f) -> p c f", c=FC if which == DOWN else C)

    def slot(k):
        return k % SLOTS

    logits_ps = gu_ps[0][0:2 * E, 0, :]
    back_ps = gu_ps[0][:, 1, 0:BT * E].rearrange("p (t e) -> p t e", t=BT)

    def steps(eng, run):
        for half in range(HALVES):
            first, last = half * STEPS, (half + 1) * STEPS - TURN
            for n in range(first - (2 if half == 0 else 0), first + TURN):
                run(At(0, TURN, n), half)
            with eng.Fori(0, (last - first) // TURN - 1) as r:
                for k in range(TURN):
                    run(At(r, TURN, first + TURN + k), half)
            for n in range(last, last + TURN):
                run(At(0, TURN, n), half)

    def stands(n):
        return not isinstance(n.r, int) or 0 <= n.k < HALVES * STEPS

    def readied(n):
        for half in range(HALVES):
            k = n.k - half * STEPS + (2 if half == 0 else NB - 1)
            if isinstance(n.r, int) and 0 <= k < NB:
                return half * NB + k
        return None

    def load_x1(sp, k):
        sp.dma_start(acc[slot(k)][:], x1_v[k]).then_inc(x1_loaded[k], DMA)

    def load_raw(sp, which, index):
        src = (g_v, u_v, d_v)[which]
        e = index if isinstance(index, int) else bass.ds(index, 1)
        src = src[e] if isinstance(index, int) else src[e].rearrange("o p c f -> (o p) c f")
        sp.dma_start(piece(w_raw, which), src).then_inc(raw_loaded[which], DMA)

    def split_hi(act, e, which):
        act.wait_ge(raw_loaded[which], e.times(DMA, DMA))
        if which != DOWN:
            wait(act, up_done, e.times(NB * FC, -NB * FC))
        else:
            wait(act, down_done, e.times(NB * BT, -NB * BT))
        act.copy(e_hi[e.parity()][:, which, :], w_raw[:, which, :]).then_inc(e_hi_made, 1)

    def split_lo(dve, e, which):
        dve.wait_ge(e_hi_made, e.times(3, which + 1))
        dve.tensor_tensor(e_lo[e.parity()][:, which, :], w_raw[:, which, :],
                          e_hi[e.parity()][:, which, :].bitcast(F32), ALU.subtract).then_inc(e_lo_made, 1)

    NORM_STEPS, NEWTON = 2 * BT + 2, 12

    def statistics(dve, k):
        at = NORM_STEPS * k
        dve.wait_ge(x1_loaded[k], DMA)
        for t in range(BT):
            dve.bn_stats(stats[:, t, :], acc[slot(k)][:, t, :]).then_inc(e_norm_chain, 1)
        dve.wait_ge(e_norm_chain, at + BT)
        wait(dve, e_xn_made, BT * k)
        for t in range(BT):
            dve.bn_aggr(mv[:, t, :], stats[:, t, :]).then_inc(e_norm_chain, 1)
        dve.wait_ge(e_norm_chain, at + 2 * BT)
        dve.tensor_scalar(var_eps[:], mv[:, :, 1], EPS, None, ALU.add).then_inc(e_norm_chain, 1)
        dve.wait_ge(e_norm_chain, at + 2 * BT + 1)
        dve.tensor_scalar(shifted[:], var_eps[:].bitcast(I32), 1, None,
                          ALU.logical_shift_right).then_inc(e_norm_chain, 1)
        dve.tensor_scalar(half_var[:], var_eps[:], -0.5, None, ALU.mult)
        dve.wait_ge(e_norm_chain, at + 2 * BT + 2)
        dve.tensor_scalar(rstd[:].bitcast(I32), shifted[:], -1.0, RSQRT_MAGIC, ALU.mult,
                          ALU.add).then_inc(e_guess_made, 1)

    def inverse_std(pool, k):
        pool.wait_ge(e_guess_made, k + 1)
        newton_rsqrt(pool, e_pool_chain, e_pool_passed, [NEWTON * k, 0], rstd[:], half_var[:], newton[:], e_rstd_made)
        pool.wait_ge(e_rstd_made, k + 1)
        pool.tensor_tensor(offset[:], mv[:, :, 0], rstd[:], ALU.mult).then_inc(e_pool_chain, 1)
        pool.wait_ge(e_pool_chain, NEWTON * (k + 1))
        pool.tensor_scalar(offset[:], offset[:], -1.0, None, ALU.mult).then_inc(e_offset_made, 1)

    def normalise(act, k):
        act.wait_ge(e_offset_made, k + 1)
        for t in range(BT):
            wait(act, e_xt_done, BT * (k - 1) + t + 1)
            act.activation(xn[t][:], acc[slot(k)][:, t, :], ACT.Identity, bias=offset[:, t:t + 1],
                           scale=rstd[:, t:t + 1]).then_inc(e_xn_made, 1)

    first_expert = At(0, U, 0)

    def start_sync(sp):
        load_x1(sp, 0)
        for which in range(3):
            load_raw(sp, which, 0)
        sp.dma_start(r_w[:], router.rearrange("(c p) e -> p c e", p=P)).then_inc(r_loaded, DMA)

    def start_scalar(act):
        for which in range(3):
            split_hi(act, first_expert, which)
        act.wait_ge(r_loaded, DMA)
        act.copy(r_parts[:, :, 0, :], r_w[:]).then_inc(r_hi_made, 1)
        normalise(act, 0)

    def start_vector(dve):
        statistics(dve, 0)
        for which in range(3):
            split_lo(dve, first_expert, which)
        dve.wait_ge(r_hi_made, 1)
        dve.tensor_tensor(r_parts[:, :, 1, :], r_w[:], r_parts[:, :, 0, :].bitcast(F32), ALU.subtract).then_inc(r_lo_made, 1)
        dve.tensor_tensor(fold[:], ident[0:2 * E, 0:E], ident[0:2 * E, E:2 * E], ALU.add).then_inc(r_lo_made, 1)

    def start_gpsimd(pool):
        pool.memset(before[:], 1.0).then_inc(before_set, 1)
        pool.wait_ge(before_set, 1)
        pool.affine_select(out=before[:], in_=before[:], compare_op=ALU.is_gt, fill=0.0, base=0,
                           pattern=[[1, E], [-1, E]], channel_multiplier=0).then_inc(before_made, 1)
        inverse_std(pool, 0)

    def build():
        with nc.Block() as block:
            @block.sync
            def _(sp):
                for k in range(1, NB):
                    if k == NB - 1:
                        sp.wait_ge(x1_stored, B * DMA)
                    load_x1(sp, k)
                for which in range(3):
                    sp.wait_ge(e_lo_made, which + 1)
                    load_raw(sp, which, 1)
                load_x1(sp, NB)

                def run(n, half):
                    if not stands(n):
                        return
                    fixed, e, blk = isinstance(n.r, int), n.over(NB), n.k % NB
                    if blk < 3 and (not fixed or e.k + 2 < HALVES * NE):
                        sp.wait_ge(e_lo_made, e.times(3, 3 + blk + 1))
                        within = At(e.r, e.step, e.k + 2 - half * NE).times(1)
                        load_raw(sp, blk, within % NE if isinstance(within, int) else within)
                    if fixed and n.k % STEPS >= STEPS - NB:
                        k = half * NB + blk
                        for t in range(BT):
                            sp.wait_ge(added, BT * n.k + t + 1)
                            sp.dma_start(out_v[k][:, t, :], acc[slot(k)][:, t, :]).then_inc(stored, DMA)
                        if half + 1 < HALVES and blk + 1 < NB:
                            sp.wait_ge(stored, DMA * BT * (blk + 1))
                            load_x1(sp, NB + blk + 1)

                steps(sp, run)
                sp.wait_ge(stored, HALVES * NB * BT * DMA)

            @block.gpsimd
            def _(pool):
                for k in range(1, HALVES * NB):
                    inverse_std(pool, k)

            @block.scalar
            def _(act):
                def rows_hi(k):
                    for t in range(BT):
                        act.wait_ge(e_xt_done, BT * k + t + 1)
                        if k >= NB and t == 0:
                            act.wait_ge(up_done, FC * (STEPS - NB + k % NB + 1))
                        act.copy(xt_hi[:, k % NB, :, t * P:(t + 1) * P],
                                 dn_ps[t][:].rearrange("p (c t) -> p c t", c=C)).then_inc(e_xt_hi_made, 1)

                def copy_logits(k):
                    act.wait_ge(logits_done, k + 1)
                    wait(act, logits_back, k)
                    act.copy(logits_t[:], logits_ps).then_inc(logits_made, 1)

                def exponentials(k):
                    act.wait_ge(shift_made, k + 1)
                    act.activation(weights[:], shift[:], ACT.Exp).then_inc(exp_made, 1)

                def hidden(n, f):
                    act.wait_ge(gate_done, n.times(FC, f + 1))
                    wait(act, h_made, n.times(FC, f + 1 - FC))
                    act.activation(silu[f][:], gu_ps[f][:, 0, :], ACT.Silu).then_inc(silu_made, 1)
                    act.wait_ge(h_made, n.times(FC, f + 1))
                    wait(act, down_done, n.times(BT, -BT))
                    act.copy(h_hi[n.parity()][:, f, :], h[f][:]).then_inc(h_hi_made, 1)

                def run(n, half):
                    k, following = readied(n), readied(n + 1)
                    if stands(n + 1):
                        hidden(n + 1, 0)
                    if k is not None:
                        rows_hi(k)
                    if stands(n + 1):
                        hidden(n + 1, 1)
                    if k is not None:
                        copy_logits(k)
                    e, blk = n.over(NB) + 1, n.k % NB
                    if stands(n) and blk < 3 and (not isinstance(n.r, int) or e.k < HALVES * NE):
                        split_hi(act, e, blk)
                    if k is not None:
                        exponentials(k)
                    if following is not None:
                        normalise(act, following)

                steps(act, run)

            @block.vector
            def _(dve):
                ROUTE_STEPS = 10

                def rows_lo(k):
                    for t in range(BT):
                        part = slice(t * P, (t + 1) * P)
                        dve.wait_ge(e_xt_hi_made, BT * k + t + 1)
                        dve.tensor_tensor(xt_lo[:, k % NB, :, part], dn_ps[t][:].rearrange("p (c t) -> p c t", c=C),
                                          xt_hi[:, k % NB, :, part].bitcast(F32), ALU.subtract).then_inc(e_xt_lo_made, 1)

                def largest(k):
                    dve.wait_ge(logits_back, k + 1)
                    dve.tensor_reduce(top[:], back_ps, AX.X, ALU.max).then_inc(route_chain, 1)
                    dve.wait_ge(route_chain, ROUTE_STEPS * k + 1)
                    dve.tensor_tensor(shift[:], back_ps, top[:].unsqueeze(2).to_broadcast([P, BT, E]),
                                      ALU.subtract).then_inc(shift_made, 1)

                def route(k):
                    count = [ROUTE_STEPS * k + 1]

                    def link(ins):
                        count[0] += 1
                        ins.then_inc(route_chain, 1)
                        dve.wait_ge(route_chain, count[0])

                    wide, pairs = [P, BT, E], [P, BT, E, E]
                    dve.wait_ge(exp_made, k + 1)
                    link(dve.tensor_reduce(total[:], weights[:], AX.X, ALU.add))
                    link(dve.reciprocal(inverse[:], total[:]))
                    link(dve.tensor_tensor(share[:], weights[:], inverse[:].unsqueeze(2).to_broadcast(wide), ALU.mult))
                    mine, others = share[:].unsqueeze(3).to_broadcast(pairs), share[:].unsqueeze(2).to_broadcast(pairs)
                    link(dve.tensor_tensor(ahead[:], others, mine, ALU.is_gt))
                    link(dve.tensor_tensor(equal[:], others, mine, ALU.is_equal))
                    link(dve.tensor_tensor(equal[:], equal[:], before[:].unsqueeze(1).to_broadcast(pairs), ALU.mult))
                    link(dve.tensor_tensor(ahead[:], ahead[:], equal[:], ALU.add))
                    link(dve.tensor_reduce(rank[:], ahead[:], AX.X, ALU.add))
                    link(dve.scalar_tensor_tensor(out=rank[:], in0=rank[:], scalar=TOP - 0.5, in1=share[:],
                                                  op0=ALU.is_lt, op1=ALU.mult))
                    dve.tensor_scalar(scale[:, k, :, 0:E], rank[:], tanh_gates[:, 1:2], None, ALU.mult).then_inc(scale_made, 1)

                def hidden(n, f):
                    dve.wait_ge(up_done, n.times(FC, f + 1))
                    dve.wait_ge(silu_made, n.times(FC, f + 1))
                    wait(dve, h_lo_made, n.times(FC, f + 1 - FC))
                    dve.tensor_tensor(h[f][:], gu_ps[f][:, 1, :], silu[f][:], ALU.mult).then_inc(h_made, 1)
                    dve.wait_ge(h_hi_made, n.times(FC, f + 1))
                    dve.tensor_tensor(h_lo[n.parity()][:, f, :], h[f][:], h_hi[n.parity()][:, f, :].bitcast(F32),
                                      ALU.subtract).then_inc(h_lo_made, 1)

                def add(n, half):
                    blk = n.k % NB
                    e = At(n.r, U, (n.k - half * STEPS) // NB).times(1)
                    k = half * NB + blk
                    wait(dve, added, n.times(BT))
                    if isinstance(e, int) and e == 0:
                        dve.wait_ge(scale_made, k + 1)
                    for t in range(BT):
                        dve.wait_ge(down_done, n.times(BT, t + 1))
                        share_of = scale[:, k, t, e:e + 1] if isinstance(e, int) else scale[:, k, t, bass.ds(e, 1)]
                        dve.scalar_tensor_tensor(out=acc[slot(k)][:, t, :], in0=dn_ps[t][:], scalar=share_of,
                                                 in1=acc[slot(k)][:, t, :], op0=ALU.mult, op1=ALU.add).then_inc(added, 1)

                def run(n, half):
                    k, following = readied(n), readied(n + 1)
                    early = following is not None and following < NB and stands(n + 1)
                    if early:
                        statistics(dve, following)
                    if stands(n + 1):
                        hidden(n + 1, 0)
                    if k is not None:
                        rows_lo(k)
                    if stands(n + 1):
                        hidden(n + 1, 1)
                    if following is not None and not early:
                        statistics(dve, following)
                    if k is not None:
                        largest(k)
                    if stands(n):
                        add(n, half)
                    if k is not None:
                        route(k)
                    e, blk = n.over(NB) + 1, n.k % NB
                    if stands(n) and blk < 3 and (not isinstance(n.r, int) or e.k < HALVES * NE):
                        split_lo(dve, e, blk)

                for k in range(HALVES * NB):
                    ins = dve.tensor_copy(scale[:, k, :, E:], tanh_gates[:, 1:2].unsqueeze(2).to_broadcast([P, BT, NE - E]))
                ins.then_inc(shared_set, 1)
                dve.wait_ge(shared_set, 1)
                dve.wait_ge(before_made, 1)
                steps(dve, run)

            @block.tensor
            def _(pe):
                def rows(n, k):
                    for t in range(BT):
                        pe.wait_ge(e_xn_made, BT * k + t + 1)
                        wait(pe, added, n.times(BT, t + 1 - BT))
                        if not stands(n + -1) and k:
                            pe.wait_ge(e_xt_lo_made, BT * (k - 1) + t + 1)
                        for c in range(C):
                            ins = pe.transpose(dn_ps[t][:, c * P:(c + 1) * P], xn[t][:, c * P:(c + 1) * P], ident[:])
                        ins.then_inc(e_xt_done, 1)

                PASSES = ((0, 0), (1, 0), (0, 1))

                def logits(n, k):
                    pe.wait_ge(e_xt_lo_made, BT * (k + 1))
                    wait(pe, h_made, (n + 1).times(FC, 1))
                    if k == 0:
                        pe.wait_ge(r_lo_made, 2)
                    for c in range(C):
                        for i, part in enumerate((xt_lo, xt_hi)):
                            ins = pe.matmul(logits_ps, r_parts[:, c].rearrange("p x e -> p (x e)"), part[:, k % NB, c, :],
                                            start=(c == 0 and i == 0), stop=(c == C - 1 and i == 1))
                    ins.then_inc(logits_done, 1)

                def transpose_back(k):
                    pe.wait_ge(logits_made, k + 1)
                    for t in range(BT):
                        ins = pe.matmul(back_ps[:, t, :], logits_t[:, t * P:(t + 1) * P], fold[:], start=True, stop=True)
                    ins.then_inc(logits_back, 1)

                def gate_up(n, f, logits_before=None):
                    e, blk = n.over(NB), n.k % NB
                    par = e.parity()
                    if blk == 0 and f == 0:
                        pe.wait_ge(e_lo_made, e.times(3, 2))
                    wait(pe, h_made, n.times(FC, f + 1 - FC))
                    for which, done in ((GATE, gate_done), (UP, up_done)):
                        if f == 0 and which == UP and logits_before is not None:
                            pe.wait_ge(shift_made, logits_before + 1)
                        hi, lo = piece(e_hi[par], which), piece(e_lo[par], which)
                        i = 0
                        for c in range(C):
                            for a, b in PASSES:
                                ins = pe.matmul(gu_ps[f][:, which, :], (hi, lo)[a][:, c, f * P:(f + 1) * P],
                                                (xt_hi, xt_lo)[b][:, blk, c, :], start=(i == 0), stop=(i == len(PASSES) * C - 1))
                                i += 1
                        ins.then_inc(done, 1)

                def down(n, k):
                    e = n.over(NB)
                    par, hp = e.parity(), n.parity()
                    if n.k % NB == 0:
                        pe.wait_ge(e_lo_made, e.times(3, 3))
                    pe.wait_ge(h_lo_made, n.times(FC, FC))
                    hi, lo = piece(e_hi[par], DOWN), piece(e_lo[par], DOWN)
                    wait(pe, added, n.times(BT))
                    for t in range(BT):
                        if k is not None:
                            pe.wait_ge(e_xt_lo_made, BT * k + t + 1)
                        i = 0
                        for f in range(FC):
                            for a, b in PASSES:
                                ins = pe.matmul(dn_ps[t][:], (h_hi, h_lo)[a][hp][:, f, t * P:(t + 1) * P], (hi, lo)[b][:, f, :],
                                                start=(i == 0), stop=(i == len(PASSES) * FC - 1))
                                i += 1
                        ins.then_inc(down_done, 1)
                        if k is not None and t == 1:
                            transpose_back(k)

                def run(n, half):
                    k = readied(n)
                    if stands(n + 1):
                        gate_up(n + 1, 0, readied(n + -1))
                    if k is not None:
                        rows(n, k)
                    if stands(n + 1):
                        gate_up(n + 1, 1)
                    if k is not None:
                        logits(n, k)
                    if stands(n):
                        down(n, k)
                    elif k is not None:
                        transpose_back(k)

                steps(pe, run)

    return Start(start_sync, start_gpsimd, start_scalar, start_vector), build


def kernel(**inputs):
    import numpy as np
    import concourse.bacc as bacc
    from concourse.bass_utils import run_bass_kernel_spmd

    a = {k: np.asarray(v) for k, v in inputs.items()}
    lay = np.ascontiguousarray

    def with_shared(experts_w, shared, axis):
        parts = np.split(shared, 2, axis=axis)
        return np.concatenate([experts_w, np.stack(parts)])

    arrays = {
        "x": a["x"].reshape(B * S, D),
        "ctx_t": lay(a["ctx_1024"].reshape(B * S, D).T),
        "g_xattn": a["g_xattn"],
        "g_ffn": a["g_ffn"],
        "wq_t": lay(a["L0_xattn_Wq"].T),
        "wk_t": lay(a["L0_xattn_Wk"].T),
        "wv_t": lay(a["L0_xattn_Wv"].T),
        "wo_t": lay(a["L0_xattn_Wo"].T),
        "bo": a["L0_xattn_bo"],
        "router": a["L0_ffn_router_w"],
        "w_gate": with_shared(a["L0_ffn_w_gate"], a["L0_ffn_ws_gate"], 1),
        "w_up": with_shared(a["L0_ffn_w_up"], a["L0_ffn_ws_up"], 1),
        "w_down": with_shared(a["L0_ffn_w_down"], a["L0_ffn_ws_down"], 0),
    }
    nc = bacc.Bacc("TRN2", target_bir_lowering=False, num_devices=1)
    aps = {k: nc.dram_tensor(f"in_{k}", v.shape, mybir.dt.from_np(v.dtype), kind="ExternalInput").ap() for k, v in arrays.items()}
    out = nc.dram_tensor("out_0", (B * S, D), F32, kind="ExternalOutput").ap()
    gated_block(nc, **aps, out=out)
    result = run_bass_kernel_spmd(nc, [{f"in_{k}": v for k, v in arrays.items()}], core_ids=[0])
    return result.results[0]["out_0"].reshape(B, S, D)
```
